# Optimizing a Trainium2 kernel written in Bass

```python
import numpy as np
import jax
import jax.numpy as jnp

def _softmax(x, axis=-1):
    return jax.nn.softmax(x, axis=axis)

def _gelu(x):
    return jax.nn.gelu(x, approximate=True)

def _silu(x):
    return jax.nn.silu(x)

def _sigmoid(x):
    return jax.nn.sigmoid(x)

def _layernorm(x, axis=-1, eps=1e-05):
    m = jnp.mean(x, axis=axis, keepdims=True)
    v = jnp.var(x, axis=axis, keepdims=True)
    return (x - m) / jnp.sqrt(v + eps)

def _scatter_add(tgt, idx, src, axis=0):
    return tgt.at[idx].add(src)

def _segment_sum(src, seg, n):
    return jax.ops.segment_sum(src, seg, n)
kernel_name = 'mk_seq_postln_d1_jaxref_r4_5884d6'

def setup_inputs(seed: int=0):
    np.random.seed(seed)
    _w = jnp.asarray

    def _L0_attn_setup():
        import jax, jax.numpy as jnp
        import numpy as np
        D_MODEL = 256
        N_STATE = 16
        D_INNER = 2 * D_MODEL
        DT_RANK = (D_MODEL + 15) // 16
        K_CONV = 4
        B, L = (1, 256)

        def _causal_dw_conv(x, w, b):
            K = w.shape[1]
            xp = jnp.pad(x, ((0, 0), (K - 1, 0), (0, 0)))
            Lx = x.shape[1]
            out = b
            for k in range(K):
                out = out + xp[:, k:k + Lx, :] * w[:, k]
            return out

        def _selective_scan(u, delta, A, Bm, Cm, D):
            dA = jnp.exp(delta[..., None] * A)
            dBu = delta[..., None] * Bm[:, :, None, :] * u[..., None]
            dA_t = jnp.moveaxis(dA, 1, 0)
            dBu_t = jnp.moveaxis(dBu, 1, 0)
            C_t = jnp.moveaxis(Cm, 1, 0)

            def step(h, inp):
                dA_i, dBu_i, C_i = inp
                h = dA_i * h + dBu_i
                y = jnp.einsum('bdn,bn->bd', h, C_i)
                return (h, y)
            h0 = jnp.zeros(u.shape[:1] + A.shape, dtype=u.dtype)
            _, ys = jax.lax.scan(step, h0, (dA_t, dBu_t, C_t))
            y = jnp.moveaxis(ys, 0, 1)
            return y + u * D
        key = jax.random.key(seed)
        ks = jax.random.split(key, 9)
        s = lambda fan_in: 1.0 / np.sqrt(fan_in)
        x = jax.random.normal(ks[0], (B, L, D_MODEL), dtype=jnp.float32)
        W_in = jax.random.normal(ks[1], (D_MODEL, 2 * D_INNER), dtype=jnp.float32) * s(D_MODEL)
        conv_w = jax.random.normal(ks[2], (D_INNER, K_CONV), dtype=jnp.float32) * s(K_CONV)
        conv_b = jnp.zeros((D_INNER,), dtype=jnp.float32)
        W_x = jax.random.normal(ks[3], (D_INNER, DT_RANK + 2 * N_STATE), dtype=jnp.float32) * s(D_INNER)
        W_dt = jax.random.normal(ks[4], (DT_RANK, D_INNER), dtype=jnp.float32) * s(DT_RANK)
        b_dt = jax.random.normal(ks[5], (D_INNER,), dtype=jnp.float32) * 0.01
        A_log = jnp.log(jnp.broadcast_to(jnp.arange(1, N_STATE + 1, dtype=jnp.float32), (D_INNER, N_STATE)))
        D = jnp.ones((D_INNER,), dtype=jnp.float32)
        W_out = jax.random.normal(ks[6], (D_INNER, D_MODEL), dtype=jnp.float32) * s(D_INNER)
        return {'x': x, 'W_in': W_in, 'conv_w': conv_w, 'conv_b': conv_b, 'W_x': W_x, 'W_dt': W_dt, 'b_dt': b_dt, 'A_log': A_log, 'D': D, 'W_out': W_out}
    _L0_attn_in = _L0_attn_setup()

    def _L0_ffn_setup():
        import jax, jax.numpy as jnp
        import numpy as np
        DIM = 256
        HIDDEN = 768
        SCALE = 1.0 / 127.0

        def _dequant(w_int, dtype):
            return w_int.astype(dtype) * jnp.asarray(SCALE, dtype)
        key = jax.random.key(seed)
        k_x, k_g, k_u, k_d = jax.random.split(key, 4)
        x = jax.random.normal(k_x, (4, 512, DIM), dtype=jnp.float32)
        w_gate = jax.random.randint(k_g, (HIDDEN, DIM), -127, 128, dtype=jnp.int32)
        w_up = jax.random.randint(k_u, (HIDDEN, DIM), -127, 128, dtype=jnp.int32)
        w_down = jax.random.randint(k_d, (DIM, HIDDEN), -127, 128, dtype=jnp.int32)
        return {'x': x, 'w_gate': w_gate, 'w_up': w_up, 'w_down': w_down}
    _L0_ffn_in = _L0_ffn_setup()
    _d = {'L0_attn_x': _L0_attn_in['x'], 'L0_attn_W_in': _L0_attn_in['W_in'], 'L0_attn_conv_w': _L0_attn_in['conv_w'], 'L0_attn_conv_b': _L0_attn_in['conv_b'], 'L0_attn_W_x': _L0_attn_in['W_x'], 'L0_attn_W_dt': _L0_attn_in['W_dt'], 'L0_attn_b_dt': _L0_attn_in['b_dt'], 'L0_attn_A_log': _L0_attn_in['A_log'], 'L0_attn_D': _L0_attn_in['D'], 'L0_attn_W_out': _L0_attn_in['W_out'], 'L0_ffn_w_gate': _L0_ffn_in['w_gate'], 'L0_ffn_w_up': _L0_ffn_in['w_up'], 'L0_ffn_w_down': _L0_ffn_in['w_down']}
    _x0 = _d['L0_attn_x']
    _d['L0_attn_x'] = jax.random.normal(jax.random.fold_in(jax.random.key(seed), 1), (4, 2048, 256), dtype=_x0.dtype)
    del _x0
    return _d

def reference(L0_attn_x, L0_attn_W_in, L0_attn_conv_w, L0_attn_conv_b, L0_attn_W_x, L0_attn_W_dt, L0_attn_b_dt, L0_attn_A_log, L0_attn_D, L0_attn_W_out, L0_ffn_w_gate, L0_ffn_w_up, L0_ffn_w_down):

    def _L0_attn_ref(x, W_in, conv_w, conv_b, W_x, W_dt, b_dt, A_log, D, W_out):
        import jax, jax.numpy as jnp
        import numpy as np
        D_MODEL = 256
        N_STATE = 16
        D_INNER = 2 * D_MODEL
        DT_RANK = (D_MODEL + 15) // 16
        K_CONV = 4
        B, L = (1, 256)

        def _causal_dw_conv(x, w, b):
            K = w.shape[1]
            xp = jnp.pad(x, ((0, 0), (K - 1, 0), (0, 0)))
            Lx = x.shape[1]
            out = b
            for k in range(K):
                out = out + xp[:, k:k + Lx, :] * w[:, k]
            return out

        def _selective_scan(u, delta, A, Bm, Cm, D):
            dA = jnp.exp(delta[..., None] * A)
            dBu = delta[..., None] * Bm[:, :, None, :] * u[..., None]
            dA_t = jnp.moveaxis(dA, 1, 0)
            dBu_t = jnp.moveaxis(dBu, 1, 0)
            C_t = jnp.moveaxis(Cm, 1, 0)

            def step(h, inp):
                dA_i, dBu_i, C_i = inp
                h = dA_i * h + dBu_i
                y = jnp.einsum('bdn,bn->bd', h, C_i)
                return (h, y)
            h0 = jnp.zeros(u.shape[:1] + A.shape, dtype=u.dtype)
            _, ys = jax.lax.scan(step, h0, (dA_t, dBu_t, C_t))
            y = jnp.moveaxis(ys, 0, 1)
            return y + u * D
        silu = jax.nn.silu
        x_and_res = x @ W_in
        x_in, res = jnp.split(x_and_res, 2, axis=-1)
        x_conv = silu(_causal_dw_conv(x_in, conv_w, conv_b))
        x_dbl = x_conv @ W_x
        dt, Bm, Cm = jnp.split(x_dbl, [DT_RANK, DT_RANK + N_STATE], axis=-1)
        delta = jax.nn.softplus(dt @ W_dt + b_dt)
        A = -jnp.exp(A_log)
        y = _selective_scan(x_conv, delta, A, Bm, Cm, D)
        return y * silu(res) @ W_out

    def _L0_ffn_ref(x, w_gate, w_up, w_down):
        import jax, jax.numpy as jnp
        import numpy as np
        DIM = 256
        HIDDEN = 768
        SCALE = 1.0 / 127.0

        def _dequant(w_int, dtype):
            return w_int.astype(dtype) * jnp.asarray(SCALE, dtype)
        wg = _dequant(w_gate, x.dtype)
        wu = _dequant(w_up, x.dtype)
        wd = _dequant(w_down, x.dtype)
        gate = jnp.einsum('bsd,hd->bsh', x, wg)
        up = jnp.einsum('bsd,hd->bsh', x, wu)
        h = jax.nn.silu(gate) * up
        return jnp.einsum('bsh,dh->bsd', h, wd)
    x = L0_attn_x
    x = _layernorm(x + _L0_attn_ref(x, L0_attn_W_in, L0_attn_conv_w, L0_attn_conv_b, L0_attn_W_x, L0_attn_W_dt, L0_attn_b_dt, L0_attn_A_log, L0_attn_D, L0_attn_W_out), axis=-1)
    x = _layernorm(x + _L0_ffn_ref(x, L0_ffn_w_gate, L0_ffn_w_up, L0_ffn_w_down), axis=-1)
    return x

_drawn_inputs = setup_inputs


def setup_inputs(seed=0):
    import zlib

    import numpy as np

    out = dict(_drawn_inputs(seed))
    spreads = {'L0_attn_conv_b': (0.0, 0.1), 'L0_attn_D': (1.0, 0.2)}
    factors = {'L0_attn_b_dt': 8.0}
    for name, (base, spread) in spreads.items():
        noise = np.random.default_rng([zlib.crc32(name.encode()), seed]).standard_normal(out[name].shape)
        drawn = base * np.exp(spread * noise) if base else spread * noise
        out[name] = jnp.asarray(drawn.astype(out[name].dtype))
    for name, factor in factors.items():
        out[name] = (out[name] * factor).astype(out[name].dtype)
    return out
```

```python
from contextlib import ExitStack

import concourse.bass as bass
from concourse import mybir

F32 = mybir.dt.float32
I32 = mybir.dt.int32
ALU = mybir.AluOpType
ACT = mybir.ActivationFunctionType

P = 128
T = 512
TT = T // P
KCONV = 4
HALO = KCONV - 1
LN_EPS = 1e-5
W_SCALE = 1.0 / 127.0
EXP_SET = "natural_log_exp_and_others"
SILU_SET = "silu_and_others"

F_FILLS = (["xin0", "xin1", "xin2", "xin3", "res0", "conv0", "res1", "conv1", "conv2", "conv3", "res2", "res3",
            "dtb", "ct", "dt0", "dt1", "dt2", "dt3"])
K_FILLS = ([f"yt{m}" for m in range(4)] + [f"o{t}" for t in range(4)] + ["x1t0", "x1t1"]
           + [f"gate{j}" for j in range(6)] + [f"up{j}" for j in range(6)] + [f"down{t}" for t in range(4)])
NF, NK = len(F_FILLS), len(K_FILLS)
F_AT = {name: n for n, name in enumerate(F_FILLS)}
K_AT = {name: n for n, name in enumerate(K_FILLS)}


def mamba_swiglu(nc, x, x_t, w_in, conv_w, conv_b, w_x, w_dt, b_dt, a_log, d_skip, w_out, w_gate_t, w_up_t,
                 w_down_t, out):
    rows, DM = x.shape
    DI = w_out.shape[0]
    NS = a_log.shape[1]
    R = w_dt.shape[0]
    HID = w_down_t.shape[0]
    SEQ = 2048
    NCH = rows // T
    PER_SEQ = SEQ // T
    KK, DB, HB = DM // P, DI // P, HID // P
    NH = NS * DB
    NHT = NS * TT
    PIECE = 4
    assert NH == NHT and DB == TT == 4 and KK == 2 and HB == 6 and NS == 16 and R == 16
    DBU = 4

    x_flat = x.rearrange("r d -> (r d)")
    out_flat = out.rearrange("r d -> (r d)")
    xt_v = x_t.rearrange("(k p) s -> p k s", p=P)
    b_rows = nc.dram_tensor("b_rows", [NS, T], F32, kind="Internal").ap()

    with ExitStack() as ctx:
        def sb(name, shape, dt=F32):
            return ctx.enter_context(nc.sbuf_tensor(name, shape, dt))

        def bank(name):
            return ctx.enter_context(nc.psum_tensor(name, [P, T], F32))

        def sem(name):
            return ctx.enter_context(nc.semaphore(name))

        win_s = sb("win_s", [P, KK, 2 * DI])
        wx_s = sb("wx_s", [P, DB, 48])
        wc_s = sb("wc_s", [P, DB, NS])
        wdt_s = sb("wdt_s", [R + 1, DI])
        wout_s = sb("wout_s", [P, DB, DM])
        wg_s = sb("wg_s", [P, KK, HID])
        wu_s = sb("wu_s", [P, KK, HID])
        wd_s = sb("wd_s", [P, HB, DM])
        convw_s = sb("convw_s", [P, DB, KCONV])
        convb_s = sb("convb_s", [P, DB])
        a_s = sb("a_s", [P, DB, NS])
        d_s = sb("d_s", [P, DB])
        diag = sb("diag", [P, DB, KCONV, P])
        ident = sb("ident", [P, P])
        eps_s = sb("eps_s", [P, 1])

        xt_s = sb("xt_s", [P, KK, T])
        xin = sb("xin", [P, DB, HALO + T + HALO])
        u = sb("u", [P, 2, DB, T])
        z = sb("z", [P, 2, DB, T])
        delta = sb("delta", [P, 2, DB, T])
        du = sb("du", [P, 2, DB, T])
        xd = sb("xd", [48, T])
        ct = sb("ct", [P, 2, TT, NS])
        brep = sb("brep", [P, 2, PIECE, T])
        dbu = sb("dbu", [P, DBU, T])
        h = sb("h", [P, 2, DB, T])
        carry = sb("carry", [P, 2, NS, DB])
        acc = sb("acc", [P, TT, DI])
        kb = sb("kb", [P, HB, T])
        xr = sb("xr", [P, 2, TT, DM])
        x1t = sb("x1t", [P, KK, T])
        bn = sb("bn", [P, TT, 6])
        mean_gap, mean2, sq = sb("mean_gap", [P, TT]), sb("mean2", [P, TT]), sb("sq", [P, TT])
        rstd = sb("rstd", [P, TT])
        nmr = sb("nmr", [P, TT])

        da = [bank(f"da{n}") for n in range(2)]
        ht = [bank(f"ht{n}") for n in range(2)]
        fp = [bank(f"fp{n}") for n in range(2)]
        kp = [bank(f"kp{n}") for n in range(2)]

        win_loaded, conv_loaded, w_loaded = sem("win_loaded"), sem("conv_loaded"), sem("w_loaded")
        ident_zero, ident_ready, tiles_set = sem("ident_zero"), sem("ident_ready"), sem("tiles_set")
        diag_ready, a_exp, a_ready, w_ready = sem("diag_ready"), sem("a_exp"), sem("a_ready"), sem("w_ready")
        da_ready, dbu_ready, h_ready = sem("da_ready"), sem("dbu_ready"), sem("h_ready")
        ht_ready, acc_done = sem("ht_ready"), sem("acc_done")
        carry_saved, carry_reset = sem("carry_saved"), sem("carry_reset")
        xt_loaded, fp_ready, xin_ready = sem("xt_loaded"), sem("fp_ready"), sem("xin_ready")
        res_raw, conv_raw, u_ready, z_ready = sem("res_raw"), sem("conv_raw"), sem("u_ready"), sem("z_ready")
        xd_ready, ct_ready, softplus_step = sem("xd_ready"), sem("ct_ready"), sem("softplus_step")
        delta_ready, du_ready, b_written = sem("delta_ready"), sem("du_ready"), sem("b_written")
        b_loaded = [sem(f"b_loaded{p}") for p in range(NS // PIECE)]
        xr_loaded = [sem(f"xr_loaded{n}") for n in range(2)]
        kp_ready, skip_done = sem("kp_ready"), sem("skip_done")
        y_ready, res1_done, x1t_ready = sem("y_ready"), sem("res1_done"), sem("x1t_ready")
        gate_raw, gate_ready, hid_ready = sem("gate_raw"), sem("gate_ready"), sem("hid_ready")
        res2_done, bn_done, stats_ready = sem("res2_done"), sem("bn_done"), sem("stats_ready")
        stats_step = sem("stats_step")
        rstd_step, nmr_ready, x1_ready = sem("rstd_step"), sem("nmr_ready"), sem("x1_ready")
        o_ready, out_stored = sem("o_ready"), sem("out_stored")

        block = ctx.enter_context(nc.Block())

        def after(eng, semaphore, value):
            if not isinstance(value, int) or value > 0:
                eng.wait_ge(semaphore, value)

        def steps(eng, step):
            step(0, 0, None)
            with eng.Fori(0, (NCH - 2) // 2) as j:
                step(2 * j + 1, 1, j)
                step(2 * j + 2, 0, j)
            step(NCH - 1, 1, None)

        @block.sync
        def _(sp):
            def load_xt(token):
                sp.dma_start(xt_s[:, :, :], xt_v[:, :, bass.ds(token, T)]).then_inc(xt_loaded, 16)

            def tokens(flat, start):
                return flat[bass.ds(start, T * DM)].rearrange("(t p d) -> p t d", p=P, t=TT)

            def load_x(c, par):
                sp.dma_start(xr[:, par, :, :], tokens(x_flat, c * (T * DM))).then_inc(xr_loaded[par], 16)

            def write_b(c):
                after(sp, b_loaded[NS // PIECE - 1], 16 * c)
                after(sp, xd_ready, 2 * c + 2)
                sp.dma_start(b_rows, xd[32:32 + NS, :]).then_inc(b_written, 16)

            def spread_b(c, p):
                if p == 0:
                    after(sp, b_written, 16 * (c + 1))
                after(sp, dbu_ready, c * NH + (p - 1) * PIECE * DB)
                sp.dma_start(brep[:, p % 2, :, :],
                             b_rows[p * PIECE:(p + 1) * PIECE, :].partition_broadcast(P)).then_inc(b_loaded[p], 16)

            load_xt(0)
            sp.dma_start(win_s[:, :, :], w_in.rearrange("(k p) n -> p k n", p=P)).then_inc(win_loaded, 16)
            sp.dma_start(convw_s[:, :, :], conv_w.rearrange("(m p) k -> p m k", p=P)).then_inc(conv_loaded, 16)
            sp.dma_start(convb_s[:, :], conv_b).then_inc(conv_loaded, 16)
            w_x_v = w_x.rearrange("(m p) n -> p m n", p=P)
            sp.dma_start(wx_s[:, :, 0:R], w_x_v[:, :, 0:R]).then_inc(w_loaded, 16)
            sp.dma_start(wx_s[:, :, 32:32 + NS], w_x_v[:, :, R:R + NS]).then_inc(w_loaded, 16)
            sp.dma_start(wc_s[:, :, :], w_x_v[:, :, R + NS:R + 2 * NS]).then_inc(w_loaded, 16)
            sp.dma_start(wdt_s[0:R, :], w_dt).then_inc(w_loaded, 16)
            sp.dma_start(wdt_s[R:R + 1, :], b_dt.rearrange("(a n) -> a n", a=1)).then_inc(w_loaded, 16)
            sp.dma_start(a_s[:, :, :], a_log.rearrange("(m p) n -> p m n", p=P)).then_inc(w_loaded, 16)
            sp.dma_start(d_s[:, :], d_skip).then_inc(w_loaded, 16)
            sp.dma_start(wout_s[:, :, :], w_out.rearrange("(m p) n -> p m n", p=P)).then_inc(w_loaded, 16)
            for tile, w in ((wg_s, w_gate_t), (wu_s, w_up_t), (wd_s, w_down_t)):
                sp.dma_start(tile[:, :, :].bitcast(I32), w.rearrange("(k p) n -> p k n", p=P)).then_inc(w_loaded, 16)
            load_x(0, 0)
            load_x(1, 1)
            after(sp, fp_ready, F_AT["res3"] + 1)
            load_xt(T)
            write_b(0)
            spread_b(0, 0)
            spread_b(0, 1)

            def step(i, par, j):
                first, last = [isinstance(i, int) and i == c for c in (0, NCH - 1)]
                spread_b(i, 2)
                spread_b(i, 3)
                if not last:
                    after(sp, fp_ready, (i + 1) * NF + F_AT["res3"] + 1)
                    load_xt((i + 2) % NCH * T)
                    write_b(i + 1)
                    spread_b(i + 1, 0)
                if not first:
                    sp.wait_ge(o_ready, TT * i)
                    sp.dma_start(tokens(out_flat, (i - 1) * (T * DM)), xr[:, 1 - par, :, :]).then_inc(out_stored, 16)
                if not last:
                    spread_b(i + 1, 1)
                if not first and not last:
                    sp.wait_ge(out_stored, 16 * i)
                    load_x(i + 1, 1 - par)

            steps(sp, step)
            after(sp, o_ready, TT * NCH)
            sp.dma_start(tokens(out_flat, (NCH - 1) * T * DM), xr[:, (NCH - 1) % 2, :, :]).then_inc(out_stored, 16)
            sp.wait_ge(xt_loaded, 16 * (NCH + 1))
            sp.wait_ge(out_stored, 16 * NCH)
            sp.wait_ge(b_written, 16 * NCH)

        @block.tensor
        def _(pe):
            f_taken = {}
            for m in range(DB):
                f_taken[f"xin{m}"] = (xin_ready, DB + 1, m + 2)
                f_taken[f"conv{m}"] = (conv_raw, DB, m + 1)
                f_taken[f"res{m}"] = (res_raw, DB, m + 1)
                f_taken[f"dt{m}"] = (delta_ready, DB, m + 1)
            f_taken["dtb"] = (xd_ready, 2, 2)
            f_taken["ct"] = (ct_ready, 1, 1)
            k_taken = {}
            for m in range(4):
                k_taken[f"yt{m}"] = (skip_done, DB, m + 1)
                k_taken[f"o{m}"] = (res1_done, TT, m + 1)
                k_taken[f"down{m}"] = (res2_done, TT, m + 1)
            for k in range(KK):
                k_taken[f"x1t{k}"] = (x1t_ready, KK, k + 1)
            for m in range(HB):
                k_taken[f"gate{m}"] = (gate_raw, HB, m + 1)
                k_taken[f"up{m}"] = (hid_ready, HB, m + 1)

            def front_bank(c, name):
                n = F_AT[name]
                s, per, count = f_taken[F_FILLS[n - 2]]
                after(pe, s, c * per + count if n >= 2 else c * per)
                return fp[n % 2]

            def back_bank(c, name):
                n = K_AT[name]
                if n >= 2:
                    s, per, count = k_taken[K_FILLS[n - 2]]
                    pe.wait_ge(s, c * per + count)
                return kp[n % 2]

            def in_proj(c, name, m):
                pe.wait_ge(xt_loaded, 16 * (c + 1))
                b = front_bank(c, name)
                for k in range(KK):
                    mm = nc.tensor.matmul(b[:, :], win_s[:, k, m * P:(m + 1) * P], xt_s[:, k, :],
                                          start=(k == 0), stop=(k == KK - 1))
                mm.then_inc(fp_ready, 1)

            def conv(c, m):
                pe.wait_ge(xin_ready, c * (DB + 1) + m + 2)
                b = front_bank(c, f"conv{m}")
                for k in range(KCONV):
                    mm = nc.tensor.matmul(b[:, :], diag[:, m, k, :], xin[:, m, k:k + T],
                                          start=(k == 0), stop=(k == KCONV - 1))
                mm.then_inc(fp_ready, 1)

            def dt_b(c, par):
                pe.wait_ge(u_ready, c + 1)
                b = front_bank(c, "dtb")
                for m in range(DB):
                    mm = nc.tensor.matmul(b[0:48, :], wx_s[:, m, :], u[:, par, m, :],
                                          start=(m == 0), stop=(m == DB - 1))
                mm.then_inc(fp_ready, 1)

            def c_rows(c, par):
                b = front_bank(c, "ct")
                for t in range(TT):
                    for m in range(DB):
                        mm = nc.tensor.matmul(b[:, t * NS:(t + 1) * NS], u[:, par, m, t * P:(t + 1) * P],
                                              wc_s[:, m, :], start=(m == 0), stop=(m == DB - 1))
                mm.then_inc(fp_ready, 1)

            def dt_proj(c, m):
                pe.wait_ge(xd_ready, 2 * c + 1)
                b = front_bank(c, f"dt{m}")
                nc.tensor.matmul(b[:, :], wdt_s[:, m * P:(m + 1) * P], xd[0:R + 1, :],
                                 start=True, stop=True).then_inc(fp_ready, 1)

            def front(c, par, s):
                for m in {0: [0, 1], 1: [2, 3]}.get(s, []):
                    in_proj(c, f"xin{m}", m)
                for m in {3: [0], 4: [1, 2], 5: [3]}.get(s, []):
                    conv(c, m)
                for m in {1: [0], 3: [1], 5: [2, 3]}.get(s, []):
                    in_proj(c, f"res{m}", DB + m)
                if s == 8:
                    dt_b(c, par)
                    c_rows(c, par)
                if s == 9:
                    for m in range(DB):
                        dt_proj(c, m)

            def back(c, par, s):
                if s == 0:
                    after(pe, acc_done, (c + 1) * NHT)
                    for m in range(DB):
                        b = back_bank(c, f"yt{m}")
                        for t in range(TT):
                            mm = nc.tensor.transpose(b[:, t * P:(t + 1) * P], acc[:, t, m * P:(m + 1) * P],
                                                     ident[:, :])
                        mm.then_inc(kp_ready, 1)
                if s == 2:
                    pe.wait_ge(y_ready, (c + 1) * DB)
                    for t in range(TT):
                        b = back_bank(c, f"o{t}")
                        for m in range(DB):
                            mm = nc.tensor.matmul(b[:, 0:DM], kb[:, m, t * P:(t + 1) * P], wout_s[:, m, :],
                                                  start=(m == 0), stop=(m == DB - 1))
                        mm.then_inc(kp_ready, 1)
                if s == 6:
                    pe.wait_ge(x1_ready, (c + 1) * TT)
                    for k in range(KK):
                        b = back_bank(c, f"x1t{k}")
                        for t in range(TT):
                            mm = nc.tensor.transpose(b[:, t * P:(t + 1) * P], xr[:, par, t, k * P:(k + 1) * P],
                                                     ident[:, :])
                        mm.then_inc(kp_ready, 1)
                for name, w, at in (("gate", wg_s, {6: [0, 1, 2], 7: [3, 4, 5]}),
                                    ("up", wu_s, {10: [0, 1, 2], 11: [3, 4, 5]})):
                    for n in at.get(s, []):
                        pe.wait_ge(x1t_ready, (c + 1) * KK)
                        b = back_bank(c, f"{name}{n}")
                        for k in range(KK):
                            mm = nc.tensor.matmul(b[:, :], w[:, k, n * P:(n + 1) * P], x1t[:, k, :],
                                                  start=(k == 0), stop=(k == KK - 1))
                        mm.then_inc(kp_ready, 1)
                for t in {12: [0, 1], 13: [2, 3]}.get(s, []):
                    pe.wait_ge(hid_ready, (c + 1) * HB)
                    b = back_bank(c, f"down{t}")
                    for n in range(HB):
                        mm = nc.tensor.matmul(b[:, 0:DM], kb[:, n, t * P:(t + 1) * P], wd_s[:, n, :],
                                              start=(n == 0), stop=(n == HB - 1))
                    mm.then_inc(kp_ready, 1)

            def turn(i, n):
                pe.wait_ge(h_ready, i * NH + (n + 1) * DB)
                for t in range(TT):
                    after(pe, acc_done, i * NHT + n * TT + t - 1)
                    for m in range(DB):
                        mm = nc.tensor.transpose(ht[t % 2][:, m * P:(m + 1) * P], h[:, n % 2, m, t * P:(t + 1) * P],
                                                 ident[:, :])
                    mm.then_inc(ht_ready, 1)

            pe.wait_ge(win_loaded, 16)
            pe.wait_ge(ident_ready, 1)
            pe.wait_ge(diag_ready, DB * KCONV)
            pe.wait_ge(w_ready, 3)
            for s in range(NS):
                front(0, 0, s)

            def step(i, par, j):
                for n in range(NS):
                    behind = not isinstance(i, int) or i > 0
                    if n == 0 and behind:
                        back(i - 1, 1 - par, 0)
                    turn(i, n)
                    if n > 0 and behind:
                        back(i - 1, 1 - par, n)
                    if not isinstance(i, int) or i < NCH - 1:
                        front(i + 1, 1 - par, n)

            steps(pe, step)
            for s in range(NS):
                back(NCH - 1, (NCH - 1) % 2, s)

        @block.scalar
        def _(act):
            def copy(dst, src):
                return nc.scalar.activation(dst, src, ACT.Copy)

            def front(c, par, s, j):
                if s == 0:
                    start = T + HALO * (j % 2) if j is not None and par == 0 else T
                    after(act, xin_ready, c * (DB + 1))
                    copy(xin[:, :, 0:HALO], xin[:, :, bass.ds(start, HALO)]).then_inc(xin_ready, 1)
                for m in {0: [0, 1], 1: [2, 3]}.get(s, []):
                    act.wait_ge(fp_ready, c * NF + F_AT[f"xin{m}"] + 1)
                    act.wait_ge(xin_ready, c * (DB + 1) + 1)
                    copy(xin[:, m, HALO:HALO + T], fp[F_AT[f"xin{m}"] % 2][:, :]).then_inc(xin_ready, 1)
                for name in {1: ["res0"], 3: ["conv0", "res1"], 4: ["conv1", "conv2"],
                             5: ["conv3", "res2", "res3"]}.get(s, []):
                    m = int(name[-1])
                    act.wait_ge(fp_ready, c * NF + F_AT[name] + 1)
                    b = fp[F_AT[name] % 2]
                    if name[:3] == "res":
                        after(act, y_ready, (c - 1) * DB)
                        copy(z[:, par, m, :], b[:, :]).then_inc(res_raw, 1)
                    else:
                        after(act, skip_done, (c - 1) * DB)
                        nc.scalar.activation(u[:, par, m, :], b[:, :], ACT.Identity,
                                             bias=convb_s[:, m:m + 1]).then_inc(conv_raw, 1)
                if s == 5:
                    nc.scalar.preload_act_table_set(SILU_SET)
                    act.wait_ge(conv_raw, (c + 1) * DB)
                    nc.scalar.activation(u[:, par, :, :], u[:, par, :, :], ACT.Silu).then_inc(u_ready, 1)
                    act.wait_ge(res_raw, (c + 1) * DB)
                    nc.scalar.activation(z[:, par, :, :], z[:, par, :, :], ACT.Silu).then_inc(z_ready, 1)
                    nc.scalar.preload_act_table_set(EXP_SET)
                if s == 8:
                    act.wait_ge(fp_ready, c * NF + F_AT["dtb"] + 1)
                    after(act, b_written, 16 * c)
                    b = fp[F_AT["dtb"] % 2]
                    copy(xd[0:R, :], b[0:R, :]).then_inc(xd_ready, 1)
                    copy(xd[32:32 + NS, :], b[32:32 + NS, :]).then_inc(xd_ready, 1)
                    act.wait_ge(fp_ready, c * NF + F_AT["ct"] + 1)
                    copy(ct[:, par, :, :], fp[F_AT["ct"] % 2][:, 0:TT * NS].rearrange("p (t n) -> p t n", n=NS))\
                        .then_inc(ct_ready, 1)
                if s == 9:
                    for q in range(2):
                        base = c * 3 * DB + 6 * q
                        for r in range(2):
                            m = 2 * q + r
                            act.wait_ge(fp_ready, c * NF + F_AT[f"dt{m}"] + 1)
                            nc.scalar.activation(delta[:, par, m, :], fp[F_AT[f"dt{m}"] % 2][:, :], ACT.Abs)\
                                .then_inc(softplus_step, 1)
                        for r in range(2):
                            d = delta[:, par, 2 * q + r, :]
                            act.wait_ge(softplus_step, base + 1 + r)
                            nc.scalar.activation(d, d, ACT.Exp, scale=-1.0).then_inc(softplus_step, 1)
                        for r in range(2):
                            d = delta[:, par, 2 * q + r, :]
                            act.wait_ge(softplus_step, base + 3 + r)
                            nc.scalar.activation(d, d, ACT.Ln, bias=1.0).then_inc(softplus_step, 1)

            def reciprocal_std(c, which):
                if which:
                    act.wait_ge(x1_ready, TT * (c + 1))
                elif isinstance(c, int):
                    after(act, o_ready, TT * c)
                act.wait_ge(stats_ready, 2 * c + which + 1)
                nc.scalar.activation(rstd[:, :], sq[:, :], ACT.Ln, bias=eps_s[:, 0:1], scale=1.0 / DM).then_inc(rstd_step, 1)
                act.wait_ge(rstd_step, 2 * (2 * c + which) + 1)
                nc.scalar.activation(rstd[:, :], rstd[:, :], ACT.Exp, scale=-0.5).then_inc(rstd_step, 1)

            def normalise(c, par, which, done):
                act.wait_ge(nmr_ready, 2 * c + which + 1)
                for t in range(TT):
                    nc.scalar.activation(xr[:, par, t, :], xr[:, par, t, :], ACT.Identity, bias=nmr[:, t:t + 1],
                                         scale=rstd[:, t:t + 1]).then_inc(done, 1)

            def back(c, par, s):
                if s == 3:
                    reciprocal_std(c, 0)
                if s == 5:
                    normalise(c, par, 0, x1_ready)
                if s == 6:
                    for k in range(KK):
                        act.wait_ge(kp_ready, c * NK + K_AT[f"x1t{k}"] + 1)
                        copy(x1t[:, k, :], kp[K_AT[f"x1t{k}"] % 2][:, :]).then_inc(x1t_ready, 1)
                for n in {6: [0, 1, 2], 7: [3, 4, 5]}.get(s, []):
                    act.wait_ge(kp_ready, c * NK + K_AT[f"gate{n}"] + 1)
                    copy(kb[:, n, :], kp[K_AT[f"gate{n}"] % 2][:, :]).then_inc(gate_raw, 1)
                if s == 7:
                    nc.scalar.preload_act_table_set(SILU_SET)
                    act.wait_ge(gate_raw, (c + 1) * HB)
                    nc.scalar.activation(kb[:, :, :], kb[:, :, :], ACT.Silu).then_inc(gate_ready, 1)
                    nc.scalar.preload_act_table_set(EXP_SET)
                if s == 13:
                    reciprocal_std(c, 1)
                if s == 14:
                    normalise(c, par, 1, o_ready)

            def exps(i, par, n):
                for m in range(DB):
                    idx = n * DB + m
                    if n == 0:
                        act.wait_ge(delta_ready, i * DB + m + 1)
                    after(act, h_ready, i * NH + idx - 1)
                    nc.scalar.activation(da[idx % 2][:, :], delta[:, par, m, :], ACT.Exp,
                                         scale=a_s[:, m, n:n + 1]).then_inc(da_ready, 1)

            nc.scalar.preload_act_table_set(EXP_SET)
            act.wait_ge(w_loaded, 16 * 11)
            nc.scalar.activation(a_s[:, :, :], a_s[:, :, :], ACT.Exp).then_inc(a_exp, 1)
            act.wait_ge(conv_loaded, 32)
            act.wait_ge(tiles_set, 5)
            for s in range(NS):
                front(0, 0, s, None)
            act.wait_ge(a_ready, 1)

            def step(i, par, j):
                for n in range(NS):
                    exps(i, par, n)
                    if n == 0:
                        continue
                    if not isinstance(i, int) or i > 0:
                        back(i - 1, 1 - par, n - 1)
                    if not isinstance(i, int) or i < NCH - 1:
                        front(i + 1, 1 - par, n - 1, j)

            steps(act, step)
            for s in range(NS):
                back(NCH - 1, (NCH - 1) % 2, s)

        @block.gpsimd
        def _(pool):
            nc.gpsimd.memset(ident[:, :], 0.0).then_inc(ident_zero, 1)
            pool.wait_ge(ident_zero, 1)
            nc.gpsimd.affine_select(out=ident[:, :], in_=ident[:, :], compare_op=ALU.not_equal, fill=1.0, base=0,
                                    pattern=[[-1, P]], channel_multiplier=1).then_inc(ident_ready, 1)

            def times_u(c, par):
                pool.wait_ge(u_ready, c + 1)
                for m in range(DB):
                    pool.wait_ge(delta_ready, c * DB + m + 1)
                    nc.gpsimd.tensor_tensor(du[:, par, m, :], delta[:, par, m, :], u[:, par, m, :], ALU.mult)\
                        .then_inc(du_ready, 1)

            def gate_y(c, par):
                pool.wait_ge(z_ready, c + 1)
                for m in range(DB):
                    pool.wait_ge(skip_done, c * DB + m + 1)
                    nc.gpsimd.tensor_tensor(kb[:, m, :], kb[:, m, :], z[:, par, m, :], ALU.mult).then_inc(y_ready, 1)

            def times_b(i, par, n):
                if n == 0:
                    pool.wait_ge(du_ready, (i + 1) * DB)
                if n % PIECE == 0:
                    pool.wait_ge(b_loaded[n // PIECE], 16 * (i + 1))
                for m in range(DB):
                    idx = n * DB + m
                    after(pool, h_ready, i * NH + idx + 1 - DBU)
                    nc.gpsimd.tensor_tensor(dbu[:, idx % DBU, :], du[:, par, m, :],
                                            brep[:, n // PIECE % 2, n % PIECE, :], ALU.mult).then_inc(dbu_ready, 1)

            times_u(0, 0)

            def step(i, par, j):
                for n in range(NS):
                    times_b(i, par, n)
                    if n == 1 and (not isinstance(i, int) or i > 0):
                        gate_y(i - 1, 1 - par)
                    if n == 11 and (not isinstance(i, int) or i < NCH - 1):
                        times_u(i + 1, 1 - par)

            steps(pool, step)
            gate_y(NCH - 1, (NCH - 1) % 2)

        @block.vector
        def _(dve):
            def front(c, par, s):
                if s == 9:
                    for m in range(DB):
                        n = F_AT[f"dt{m}"]
                        dve.wait_ge(fp_ready, c * NF + n + 1)
                        dve.wait_ge(softplus_step, c * 3 * DB + 6 * (m // 2) + 5 + m % 2)
                        d = delta[:, par, m, :]
                        nc.vector.scalar_tensor_tensor(out=d, in0=fp[n % 2][:, :], scalar=0.0, in1=d, op0=ALU.max,
                                                       op1=ALU.add).then_inc(delta_ready, 1)

            def residual(c, par, name, t, done):
                n = K_AT[f"{name}{t}"]
                dve.wait_ge(kp_ready, c * NK + n + 1)
                nc.vector.tensor_tensor(xr[:, par, t, :], kp[n % 2][:, 0:DM], xr[:, par, t, :], ALU.add)\
                    .then_inc(done, 1)

            def statistics(c, par, which, done):
                if which:
                    dve.wait_ge(nmr_ready, 2 * c + 1)
                for t in range(TT):
                    dve.wait_ge(done, c * TT + t + 1)
                    nc.vector.bn_stats(bn[:, t, :], xr[:, par, t, :]).then_inc(bn_done, 1)
                base = 4 * (2 * c + which)
                dve.wait_ge(bn_done, base + TT)
                nc.vector.tensor_tensor(mean_gap[:, :], bn[:, :, 1], bn[:, :, 4], ALU.subtract).then_inc(stats_step, 1)
                nc.vector.tensor_tensor(mean2[:, :], bn[:, :, 1], bn[:, :, 4], ALU.add).then_inc(stats_step, 1)
                nc.vector.tensor_tensor(sq[:, :], bn[:, :, 2], bn[:, :, 5], ALU.add).then_inc(stats_step, 1)
                dve.wait_ge(stats_step, base + 1)
                nc.vector.scalar_tensor_tensor(out=mean_gap[:, :], in0=mean_gap[:, :], scalar=DM / 4.0,
                                               in1=mean_gap[:, :], op0=ALU.mult, op1=ALU.mult).then_inc(stats_step, 1)
                dve.wait_ge(stats_step, base + 4)
                nc.vector.tensor_tensor(sq[:, :], sq[:, :], mean_gap[:, :], ALU.add).then_inc(stats_ready, 1)

            def shift(c, which):
                dve.wait_ge(rstd_step, 2 * (2 * c + which + 1))
                nc.vector.scalar_tensor_tensor(out=nmr[:, :], in0=mean2[:, :], scalar=-0.5, in1=rstd[:, :],
                                               op0=ALU.mult, op1=ALU.mult).then_inc(nmr_ready, 1)

            def back(c, par, s):
                if s == 0:
                    for m in range(DB):
                        n = K_AT[f"yt{m}"]
                        dve.wait_ge(kp_ready, c * NK + n + 1)
                        nc.vector.scalar_tensor_tensor(out=kb[:, m, :], in0=u[:, par, m, :], scalar=d_s[:, m:m + 1],
                                                       in1=kp[n % 2][:, :], op0=ALU.mult, op1=ALU.add)\
                            .then_inc(skip_done, 1)
                if s == 2:
                    dve.wait_ge(xr_loaded[par], 8 * (c - par) + 16)
                    for t in range(TT):
                        residual(c, par, "o", t, res1_done)
                    statistics(c, par, 0, res1_done)
                if s == 4:
                    shift(c, 0)
                for m in {10: [0, 1, 2], 11: [3, 4, 5]}.get(s, []):
                    n = K_AT[f"up{m}"]
                    dve.wait_ge(gate_ready, c + 1)
                    dve.wait_ge(kp_ready, c * NK + n + 1)
                    nc.vector.tensor_tensor(kb[:, m, :], kp[n % 2][:, :], kb[:, m, :], ALU.mult)\
                        .then_inc(hid_ready, 1)
                for t in {12: [0, 1], 13: [2, 3]}.get(s, []):
                    residual(c, par, "down", t, res2_done)
                if s == 13:
                    statistics(c, par, 1, res2_done)
                if s == 14:
                    shift(c, 1)

            def scan(i, n):
                for m in range(DB):
                    idx = n * DB + m
                    dve.wait_ge(da_ready, i * NH + idx + 1)
                    dve.wait_ge(dbu_ready, i * NH + idx + 1)
                    after(dve, ht_ready, i * NHT + (n - 1) * TT)
                    after(dve, carry_saved, i * NS + n - 1)
                    nc.vector.tensor_tensor_scan(h[:, n % 2, m, :], da[idx % 2][:, :], dbu[:, idx % DBU, :],
                                                 carry[:, 1, n, m:m + 1], ALU.mult, ALU.add).then_inc(h_ready, 1)

            def save_carry(i, n):
                dve.wait_ge(h_ready, i * NH + (n + 1) * DB)
                nc.vector.tensor_copy(carry[:, 1, n, :], h[:, n % 2, :, T - 1]).then_inc(carry_saved, 1)

            def sum_states(i, par, n):
                for t in range(TT):
                    g = i * NHT + n * TT + t
                    dve.wait_ge(ht_ready, g + 1)
                    c_col = ct[:, par, t, n:n + 1]
                    if n == 0:
                        dve.wait_ge(ct_ready, i + 1)
                        after(dve, kp_ready, (i - 1) * NK + K_AT["yt3"] + 1)
                        ins = nc.vector.tensor_scalar(acc[:, t, :], ht[t % 2][:, :], c_col, None, ALU.mult)
                    else:
                        dve.wait_ge(acc_done, g + 1 - TT)
                        ins = nc.vector.scalar_tensor_tensor(out=acc[:, t, :], in0=ht[t % 2][:, :], scalar=c_col,
                                                             in1=acc[:, t, :], op0=ALU.mult, op1=ALU.add)
                    ins.then_inc(acc_done, 1)

            nc.vector.memset(carry[:, :, :, :], 0.0).then_inc(tiles_set, 1)
            nc.vector.memset(xin[:, :, T:T + 2 * HALO], 0.0).then_inc(tiles_set, 1)
            nc.vector.memset(xd[0:32, :], 1.0).then_inc(tiles_set, 1)
            nc.vector.memset(wx_s[:, :, R:32], 0.0).then_inc(tiles_set, 1)
            nc.vector.memset(eps_s[:, :], LN_EPS).then_inc(tiles_set, 1)
            dve.wait_ge(tiles_set, 5)
            dve.wait_ge(ident_ready, 1)
            dve.wait_ge(conv_loaded, 32)
            for m in range(DB):
                for k in range(KCONV):
                    nc.vector.tensor_scalar(diag[:, m, k, :], ident[:, :], convw_s[:, m, k:k + 1], None, ALU.mult)\
                        .then_inc(diag_ready, 1)
            dve.wait_ge(w_loaded, 16 * 11)
            for w in (wg_s, wu_s, wd_s):
                nc.vector.tensor_scalar(w[:, :, :], w[:, :, :].bitcast(I32), W_SCALE, None, ALU.mult)\
                    .then_inc(w_ready, 1)
            dve.wait_ge(a_exp, 1)
            nc.vector.tensor_scalar(a_s[:, :, :], a_s[:, :, :], -1.0, None, ALU.mult).then_inc(a_ready, 1)
            front(0, 0, 9)

            def step(i, par, j):
                first = isinstance(i, int) and i == 0
                if not first:
                    save_carry(i - 1, NS - 1)
                if j is not None and par == 0:
                    dve.wait_ge(carry_saved, i * NS)
                    nc.vector.tensor_copy(carry[:, 1, :, :], carry[:, bass.ds((j + 1) % 2, 1), :, :])\
                        .then_inc(carry_reset, 1)
                    dve.wait_ge(carry_reset, j + 1)
                for n in range(NS):
                    scan(i, n)
                    if n == 0:
                        if not first:
                            sum_states(i - 1, 1 - par, NS - 1)
                        continue
                    save_carry(i, n - 1)
                    if n == 1 and not first:
                        back(i - 1, 1 - par, 0)
                    sum_states(i, par, n - 1)
                    if n > 1 and not first:
                        back(i - 1, 1 - par, n - 1)
                    if not isinstance(i, int) or i < NCH - 1:
                        front(i + 1, 1 - par, n - 1)

            steps(dve, step)
            sum_states(NCH - 1, (NCH - 1) % 2, NS - 1)
            for s in range(NS):
                back(NCH - 1, (NCH - 1) % 2, s)


def kernel(L0_attn_x, L0_attn_W_in, L0_attn_conv_w, L0_attn_conv_b, L0_attn_W_x, L0_attn_W_dt, L0_attn_b_dt,
           L0_attn_A_log, L0_attn_D, L0_attn_W_out, L0_ffn_w_gate, L0_ffn_w_up, L0_ffn_w_down):
    import numpy as np
    import concourse.bacc as bacc
    from concourse import mybir as mb
    from concourse.bass_utils import run_bass_kernel_spmd

    x = np.ascontiguousarray(L0_attn_x)
    rows = x.reshape(-1, x.shape[-1])
    arrays = {
        "x": rows, "x_t": np.ascontiguousarray(rows.T),
        "w_in": L0_attn_W_in, "conv_w": L0_attn_conv_w, "conv_b": np.asarray(L0_attn_conv_b).reshape(-1, P).T, "w_x": L0_attn_W_x,
        "w_dt": L0_attn_W_dt, "b_dt": L0_attn_b_dt, "a_log": L0_attn_A_log, "d_skip": np.asarray(L0_attn_D).reshape(-1, P).T,
        "w_out": L0_attn_W_out,
        "w_gate_t": np.asarray(L0_ffn_w_gate).T, "w_up_t": np.asarray(L0_ffn_w_up).T,
        "w_down_t": np.asarray(L0_ffn_w_down).T,
    }
    arrays = {name: np.ascontiguousarray(a) for name, a in arrays.items()}
    nc = bacc.Bacc("TRN2", target_bir_lowering=False, num_devices=1)
    args = [nc.dram_tensor(name, a.shape, mb.dt.from_np(a.dtype), kind="ExternalInput").ap()
            for name, a in arrays.items()]
    out = nc.dram_tensor("out", rows.shape, mb.dt.from_np(rows.dtype), kind="ExternalOutput").ap()
    mamba_swiglu(nc, *args, out)
    result = run_bass_kernel_spmd(nc, [arrays], core_ids=[0])
    return result.results[0]["out"].reshape(x.shape)
```

```python
from contextlib import ExitStack

import concourse.bass as bass
from concourse import mybir

F32 = mybir.dt.float32
I32 = mybir.dt.int32
ALU = mybir.AluOpType
ACT = mybir.ActivationFunctionType

P = 128
T = 512
TT = T // P
KCONV = 4
HALO = KCONV - 1
LN_EPS = 1e-5
W_SCALE = 1.0 / 127.0
EXP_SET = "natural_log_exp_and_others"
SILU_SET = "silu_and_others"

FRONT_AT = {"xin0": 0, "xin1": 1, "xin2": 2, "xin3": 4, "conv0": 5, "res0": 9, "conv1": 10, "res1": 13, "conv2": 14,
            "res2": 17, "conv3": 18, "res3": 21, "dtb": 28, "ct": 30, "dt0": 32, "dt1": 33, "dt2": 43, "dt3": 44}
BACK_AT = {"yt0": 5, "yt1": 6, "yt2": 7, "yt3": 8, "o0": 22, "o1": 24, "o2": 25, "o3": 26, "x1t0": 33, "x1t1": 33,
           "gate0": 34, "gate1": 35, "gate2": 37, "gate3": 38, "gate4": 39, "gate5": 41,
           "up0": 46, "up1": 47, "up2": 48, "up3": 50, "up4": 51, "up5": 52,
           "down0": 53, "down1": 55, "down2": 57, "down3": 58}
STATS1, RSTD1, SHIFT1, NORM1 = 28, 29, 30, 31
STATS2, RSTD2, SHIFT2, NORM2 = 60, 61, 62, 63
SILU_FRONT, SILU_BACK = 23, 43
AHEAD = 4
GATE_Y, TIMES_U = 9, 50
F_FILLS, K_FILLS = list(FRONT_AT), list(BACK_AT)
NF, NK = len(F_FILLS), len(K_FILLS)
F_AT = {name: n for n, name in enumerate(F_FILLS)}
K_AT = {name: n for n, name in enumerate(K_FILLS)}


def mamba_swiglu(nc, x, x_t, w_in, conv_w, conv_b, w_x, w_dt, b_dt, a_log, d_skip, w_out, w_gate_t, w_up_t,
                 w_down_t, out):
    rows, DM = x.shape
    DI = w_out.shape[0]
    NS = a_log.shape[1]
    R = w_dt.shape[0]
    HID = w_down_t.shape[0]
    SEQ = 2048
    NCH = rows // T
    PER_SEQ = SEQ // T
    KK, DB, HB = DM // P, DI // P, HID // P
    NH = NS * DB
    NHT = NS * TT
    PIECE = 2
    NB = NS // PIECE
    assert NH == NHT and DB == TT == 4 and KK == 2 and HB == 6 and NS == 16 and R == 16
    DBU = 4

    x_flat = x.rearrange("r d -> (r d)")
    out_flat = out.rearrange("r d -> (r d)")
    xt_v = x_t.rearrange("(k p) s -> p k s", p=P)
    b_rows = nc.dram_tensor("b_rows", [NS, T], F32, kind="Internal").ap()

    with ExitStack() as ctx:
        def sb(name, shape, dt=F32):
            return ctx.enter_context(nc.sbuf_tensor(name, shape, dt))

        def bank(name):
            return ctx.enter_context(nc.psum_tensor(name, [P, T], F32))

        def sem(name):
            return ctx.enter_context(nc.semaphore(name))

        win_s = sb("win_s", [P, KK, 2 * DI])
        wx_s = sb("wx_s", [P, DB, 48])
        wc_s = sb("wc_s", [P, DB, NS])
        wdt_s = sb("wdt_s", [R + 1, DI])
        wout_s = sb("wout_s", [P, DB, DM])
        wg_s = sb("wg_s", [P, KK, HID])
        wu_s = sb("wu_s", [P, KK, HID])
        wd_s = sb("wd_s", [P, HB, DM])
        convw_s = sb("convw_s", [P, DB, KCONV])
        convb_s = sb("convb_s", [P, DB])
        a_s = sb("a_s", [P, DB, NS])
        d_s = sb("d_s", [P, DB])
        diag = sb("diag", [P, DB, KCONV, P])
        ident = sb("ident", [P, P])
        eps_s = sb("eps_s", [P, 1])

        xt_s = sb("xt_s", [P, KK, T])
        xin = sb("xin", [P, DB, HALO + T + HALO])
        u = sb("u", [P, 2, DB, T])
        z = sb("z", [P, 2, DB, T])
        delta = sb("delta", [P, 2, DB, T])
        du = sb("du", [P, 2, DB, T])
        xd = sb("xd", [48, T])
        ct = sb("ct", [P, 2, TT, NS])
        brep = sb("brep", [P, 2, PIECE, T])
        dbu = sb("dbu", [P, DBU, T])
        da_ahead = sb("da_ahead", [P, AHEAD, T])
        h = sb("h", [P, 2, DB, T])
        carry = sb("carry", [P, 2, NS, DB])
        acc = sb("acc", [P, 2, TT, DI])
        kb = sb("kb", [P, HB, T])
        xr = sb("xr", [P, 2, TT, DM])
        x1t = sb("x1t", [P, KK, T])
        bn = sb("bn", [P, TT, 6])
        mean_gap, mean2, sq = sb("mean_gap", [P, TT]), sb("mean2", [P, TT]), sb("sq", [P, TT])
        rstd = sb("rstd", [P, TT])
        nmr = sb("nmr", [P, TT])

        da = [bank(f"da{n}") for n in range(2)]
        ht = [bank(f"ht{n}") for n in range(2)]
        fp = [bank(f"fp{n}") for n in range(2)]
        kp = [bank(f"kp{n}") for n in range(2)]

        win_loaded, conv_loaded, w_loaded = sem("win_loaded"), sem("conv_loaded"), sem("w_loaded")
        ident_zero, ident_ready, tiles_set = sem("ident_zero"), sem("ident_ready"), sem("tiles_set")
        diag_ready, a_exp, a_ready, w_ready = sem("diag_ready"), sem("a_exp"), sem("a_ready"), sem("w_ready")
        da_ready, dbu_ready, h_ready = sem("da_ready"), sem("dbu_ready"), sem("h_ready")
        ht_ready, acc_done = sem("ht_ready"), sem("acc_done")
        carry_saved, carry_reset = sem("carry_saved"), sem("carry_reset")
        xt_loaded, fp_ready, xin_ready = sem("xt_loaded"), sem("fp_ready"), sem("xin_ready")
        res_raw, conv_raw, u_ready, z_ready = sem("res_raw"), sem("conv_raw"), sem("u_ready"), sem("z_ready")
        xd_ready, ct_ready, softplus_step = sem("xd_ready"), sem("ct_ready"), sem("softplus_step")
        delta_ready, du_ready, b_written = sem("delta_ready"), sem("du_ready"), sem("b_written")
        b_loaded = [sem(f"b_loaded{n}") for n in range(2)]
        xr_loaded = [sem(f"xr_loaded{n}") for n in range(2)]
        kp_ready, skip_done = sem("kp_ready"), sem("skip_done")
        y_ready, res1_done, x1t_ready = sem("y_ready"), sem("res1_done"), sem("x1t_ready")
        gate_raw, gate_ready, hid_ready = sem("gate_raw"), sem("gate_ready"), sem("hid_ready")
        res2_done, bn_done, stats_ready = sem("res2_done"), sem("bn_done"), sem("stats_ready")
        stats_step = sem("stats_step")
        rstd_step, nmr_ready, x1_ready = sem("rstd_step"), sem("nmr_ready"), sem("x1_ready")
        o_ready, out_stored = sem("o_ready"), sem("out_stored")

        block = ctx.enter_context(nc.Block())

        def after(eng, semaphore, value):
            if not isinstance(value, int) or value > 0:
                eng.wait_ge(semaphore, value)

        def fills(at, beat):
            return [name for name, b in at.items() if b == beat]

        def ahead(beat):
            for start in (SILU_FRONT, SILU_BACK):
                if start < beat <= start + AHEAD:
                    return beat - start - 1
            return None

        def steps(eng, step):
            step(0, 0, None)
            with eng.Fori(0, (NCH - 2) // 2) as j:
                step(2 * j + 1, 1, j)
                step(2 * j + 2, 0, j)
            step(NCH - 1, 1, None)

        @block.sync
        def _(sp):
            def load_xt(token):
                sp.dma_start(xt_s[:, :, :], xt_v[:, :, bass.ds(token, T)]).then_inc(xt_loaded, 16)

            def tokens(flat, start):
                return flat[bass.ds(start, T * DM)].rearrange("(t p d) -> p t d", p=P, t=TT)

            def load_x(c, par):
                sp.dma_start(xr[:, par, :, :], tokens(x_flat, c * (T * DM))).then_inc(xr_loaded[par], 16)

            def write_b(c):
                for half in range(2):
                    after(sp, b_loaded[half], 8 * NB * c)
                after(sp, xd_ready, 2 * c + 2)
                sp.dma_start(b_rows, xd[32:32 + NS, :]).then_inc(b_written, 16)

            def spread_b(c, p, later=0):
                if p == 0:
                    after(sp, b_written, c * 16 + 16 * (later + 1))
                else:
                    after(sp, dbu_ready, c * NH + (later * NH + (p - 1) * PIECE * DB))
                sp.dma_start(brep[:, p % 2, :, :],
                             b_rows[p * PIECE:(p + 1) * PIECE, :].partition_broadcast(P)).then_inc(b_loaded[p % 2], 16)

            load_xt(0)
            sp.dma_start(win_s[:, :, :], w_in.rearrange("(k p) n -> p k n", p=P)).then_inc(win_loaded, 16)
            sp.dma_start(convw_s[:, :, :], conv_w.rearrange("(m p) k -> p m k", p=P)).then_inc(conv_loaded, 16)
            sp.dma_start(convb_s[:, :], conv_b).then_inc(conv_loaded, 16)
            w_x_v = w_x.rearrange("(m p) n -> p m n", p=P)
            sp.dma_start(wx_s[:, :, 0:R], w_x_v[:, :, 0:R]).then_inc(w_loaded, 16)
            sp.dma_start(wx_s[:, :, 32:32 + NS], w_x_v[:, :, R:R + NS]).then_inc(w_loaded, 16)
            sp.dma_start(wc_s[:, :, :], w_x_v[:, :, R + NS:R + 2 * NS]).then_inc(w_loaded, 16)
            sp.dma_start(wdt_s[0:R, :], w_dt).then_inc(w_loaded, 16)
            sp.dma_start(wdt_s[R:R + 1, :], b_dt.rearrange("(a n) -> a n", a=1)).then_inc(w_loaded, 16)
            sp.dma_start(a_s[:, :, :], a_log.rearrange("(m p) n -> p m n", p=P)).then_inc(w_loaded, 16)
            sp.dma_start(d_s[:, :], d_skip).then_inc(w_loaded, 16)
            sp.dma_start(wout_s[:, :, :], w_out.rearrange("(m p) n -> p m n", p=P)).then_inc(w_loaded, 16)
            for tile, w in ((wg_s, w_gate_t), (wu_s, w_up_t), (wd_s, w_down_t)):
                sp.dma_start(tile[:, :, :].bitcast(I32), w.rearrange("(k p) n -> p k n", p=P)).then_inc(w_loaded, 16)
            load_x(0, 0)
            load_x(1, 1)
            after(sp, fp_ready, F_AT["res3"] + 1)
            load_xt(T)
            write_b(0)
            spread_b(0, 0)
            spread_b(0, 1)

            def step(i, par, j):
                first, last = [isinstance(i, int) and i == c for c in (0, NCH - 1)]
                for p in range(2, NB):
                    spread_b(i, p)
                if not last:
                    write_b(i + 1)
                    after(sp, dbu_ready, i * NH + (NB - 1) * PIECE * DB)
                    load_xt((i + 2) % NCH * T)
                    spread_b(i, 0, 1)
                    spread_b(i, 1, 1)
                if not first:
                    sp.wait_ge(o_ready, TT * i)
                    sp.dma_start(tokens(out_flat, (i - 1) * (T * DM)), xr[:, 1 - par, :, :]).then_inc(out_stored, 16)
                if not first and not last:
                    sp.wait_ge(out_stored, 16 * i)
                    load_x(i + 1, 1 - par)

            steps(sp, step)
            after(sp, o_ready, TT * NCH)
            sp.dma_start(tokens(out_flat, (NCH - 1) * T * DM), xr[:, (NCH - 1) % 2, :, :]).then_inc(out_stored, 16)
            sp.wait_ge(xt_loaded, 16 * (NCH + 1))
            sp.wait_ge(out_stored, 16 * NCH)
            sp.wait_ge(b_written, 16 * NCH)

        @block.tensor
        def _(pe):
            f_taken = {}
            for m in range(DB):
                f_taken[f"xin{m}"] = (xin_ready, DB + 1, m + 2)
                f_taken[f"conv{m}"] = (conv_raw, DB, m + 1)
                f_taken[f"res{m}"] = (res_raw, DB, m + 1)
                f_taken[f"dt{m}"] = (delta_ready, DB, m + 1)
            f_taken["dtb"] = (xd_ready, 2, 2)
            f_taken["ct"] = (ct_ready, 1, 1)
            k_taken = {}
            for m in range(4):
                k_taken[f"yt{m}"] = (skip_done, DB, m + 1)
                k_taken[f"o{m}"] = (res1_done, TT, m + 1)
                k_taken[f"down{m}"] = (res2_done, TT, m + 1)
            for k in range(KK):
                k_taken[f"x1t{k}"] = (x1t_ready, KK, k + 1)
            for m in range(HB):
                k_taken[f"gate{m}"] = (gate_raw, HB, m + 1)
                k_taken[f"up{m}"] = (hid_ready, HB, m + 1)

            def front_bank(c, name):
                n = F_AT[name]
                s, per, count = f_taken[F_FILLS[n - 2]]
                after(pe, s, c * per + count if n >= 2 else c * per)
                return fp[n % 2]

            def back_bank(c, name):
                n = K_AT[name]
                if n >= 2:
                    s, per, count = k_taken[K_FILLS[n - 2]]
                    pe.wait_ge(s, c * per + count)
                return kp[n % 2]

            def in_proj(c, name, m):
                pe.wait_ge(xt_loaded, 16 * (c + 1))
                b = front_bank(c, name)
                for k in range(KK):
                    mm = nc.tensor.matmul(b[:, :], win_s[:, k, m * P:(m + 1) * P], xt_s[:, k, :],
                                          start=(k == 0), stop=(k == KK - 1))
                mm.then_inc(fp_ready, 1)

            def conv(c, m):
                pe.wait_ge(xin_ready, c * (DB + 1) + m + 2)
                b = front_bank(c, f"conv{m}")
                for k in range(KCONV):
                    mm = nc.tensor.matmul(b[:, :], diag[:, m, k, :], xin[:, m, k:k + T],
                                          start=(k == 0), stop=(k == KCONV - 1))
                mm.then_inc(fp_ready, 1)

            def dt_b(c, par):
                pe.wait_ge(u_ready, c + 1)
                b = front_bank(c, "dtb")
                for m in range(DB):
                    mm = nc.tensor.matmul(b[0:48, :], wx_s[:, m, :], u[:, par, m, :],
                                          start=(m == 0), stop=(m == DB - 1))
                mm.then_inc(fp_ready, 1)

            def c_rows(c, par):
                b = front_bank(c, "ct")
                for t in range(TT):
                    for m in range(DB):
                        mm = nc.tensor.matmul(b[:, t * NS:(t + 1) * NS], u[:, par, m, t * P:(t + 1) * P],
                                              wc_s[:, m, :], start=(m == 0), stop=(m == DB - 1))
                mm.then_inc(fp_ready, 1)

            def dt_proj(c, m):
                pe.wait_ge(xd_ready, 2 * c + 1)
                b = front_bank(c, f"dt{m}")
                nc.tensor.matmul(b[:, :], wdt_s[:, m * P:(m + 1) * P], xd[0:R + 1, :],
                                 start=True, stop=True).then_inc(fp_ready, 1)

            def front(c, par, beat):
                for name in fills(FRONT_AT, beat):
                    m = int(name[-1]) if name[-1].isdigit() else 0
                    if name[:3] == "xin":
                        in_proj(c, name, m)
                    elif name[:3] == "res":
                        in_proj(c, name, DB + m)
                    elif name[:4] == "conv":
                        conv(c, m)
                    elif name == "dtb":
                        dt_b(c, par)
                    elif name == "ct":
                        c_rows(c, par)
                    else:
                        dt_proj(c, m)

            def turn_sum(c, par, m):
                pe.wait_ge(acc_done, (c + 1) * NHT)
                b = back_bank(c, f"yt{m}")
                for t in range(TT):
                    mm = nc.tensor.transpose(b[:, t * P:(t + 1) * P], acc[:, par, t, m * P:(m + 1) * P], ident[:, :])
                mm.then_inc(kp_ready, 1)

            def out_proj(c, t):
                pe.wait_ge(y_ready, (c + 1) * DB)
                b = back_bank(c, f"o{t}")
                for m in range(DB):
                    mm = nc.tensor.matmul(b[:, 0:DM], kb[:, m, t * P:(t + 1) * P], wout_s[:, m, :],
                                          start=(m == 0), stop=(m == DB - 1))
                mm.then_inc(kp_ready, 1)

            def turn_x1(c, par, k):
                pe.wait_ge(x1_ready, (c + 1) * TT)
                b = back_bank(c, f"x1t{k}")
                for t in range(TT):
                    mm = nc.tensor.transpose(b[:, t * P:(t + 1) * P], xr[:, par, t, k * P:(k + 1) * P], ident[:, :])
                mm.then_inc(kp_ready, 1)

            def hidden(c, name, w, n):
                pe.wait_ge(x1t_ready, (c + 1) * KK)
                b = back_bank(c, name)
                for k in range(KK):
                    mm = nc.tensor.matmul(b[:, :], w[:, k, n * P:(n + 1) * P], x1t[:, k, :],
                                          start=(k == 0), stop=(k == KK - 1))
                mm.then_inc(kp_ready, 1)

            def down(c, t):
                pe.wait_ge(hid_ready, (c + 1) * HB)
                b = back_bank(c, f"down{t}")
                for n in range(HB):
                    mm = nc.tensor.matmul(b[:, 0:DM], kb[:, n, t * P:(t + 1) * P], wd_s[:, n, :],
                                          start=(n == 0), stop=(n == HB - 1))
                mm.then_inc(kp_ready, 1)

            def back(c, par, beat):
                for name in fills(BACK_AT, beat):
                    n = int(name[-1])
                    if name[:2] == "yt":
                        turn_sum(c, par, n)
                    elif name[:3] == "x1t":
                        turn_x1(c, par, n)
                    elif name[0] == "o":
                        out_proj(c, n)
                    elif name[:4] == "gate":
                        hidden(c, name, wg_s, n)
                    elif name[:2] == "up":
                        hidden(c, name, wu_s, n)
                    else:
                        down(c, n)

            def turn(i, q):
                n, t = q // TT, q % TT
                pe.wait_ge(h_ready, i * NH + (n + 1) * DB)
                after(pe, acc_done, i * NHT + q - 1)
                for m in range(DB):
                    mm = nc.tensor.transpose(ht[q % 2][:, m * P:(m + 1) * P], h[:, n % 2, m, t * P:(t + 1) * P],
                                             ident[:, :])
                mm.then_inc(ht_ready, 1)

            pe.wait_ge(win_loaded, 16)
            pe.wait_ge(ident_ready, 1)
            pe.wait_ge(diag_ready, DB * KCONV)
            pe.wait_ge(w_ready, 3)
            for beat in range(NH):
                front(0, 0, beat)

            def step(i, par, j):
                first, last = [isinstance(i, int) and i == c for c in (0, NCH - 1)]
                for beat in range(NH):
                    if beat >= DB:
                        turn(i, beat - DB)
                    elif not first:
                        turn(i - 1, NHT - DB + beat)
                    if not first:
                        back(i - 1, 1 - par, beat)
                    if not last:
                        front(i + 1, 1 - par, beat)

            steps(pe, step)
            for q in range(NHT - DB, NHT):
                turn(NCH - 1, q)
            for beat in range(NH):
                back(NCH - 1, (NCH - 1) % 2, beat)

        @block.scalar
        def _(act):
            def copy(dst, src):
                return nc.scalar.activation(dst, src, ACT.Copy)

            def front(c, par, beat, j):
                if beat == 0:
                    start = T + HALO * (j % 2) if j is not None and par == 0 else T
                    after(act, xin_ready, c * (DB + 1))
                    copy(xin[:, :, 0:HALO], xin[:, :, bass.ds(start, HALO)]).then_inc(xin_ready, 1)
                for name in fills(FRONT_AT, beat - 1):
                    m = int(name[-1]) if name[-1].isdigit() else 0
                    b = fp[F_AT[name] % 2]
                    act.wait_ge(fp_ready, c * NF + F_AT[name] + 1)
                    if name[:3] == "xin":
                        act.wait_ge(xin_ready, c * (DB + 1) + 1)
                        copy(xin[:, m, HALO:HALO + T], b[:, :]).then_inc(xin_ready, 1)
                    elif name[:3] == "res":
                        after(act, y_ready, (c - 2) * DB + m + 1)
                        copy(z[:, par, m, :], b[:, :]).then_inc(res_raw, 1)
                    elif name[:4] == "conv":
                        after(act, skip_done, (c - 2) * DB + m + 1)
                        nc.scalar.activation(u[:, par, m, :], b[:, :], ACT.Identity,
                                             bias=convb_s[:, m:m + 1]).then_inc(conv_raw, 1)
                    elif name == "dtb":
                        after(act, b_written, 16 * c)
                        copy(xd[0:R, :], b[0:R, :]).then_inc(xd_ready, 1)
                        copy(xd[32:32 + NS, :], b[32:32 + NS, :]).then_inc(xd_ready, 1)
                    elif name == "ct":
                        copy(ct[:, par, :, :], b[:, 0:TT * NS].rearrange("p (t n) -> p t n", n=NS))\
                            .then_inc(ct_ready, 1)
                    else:
                        d = delta[:, par, m, :]
                        done = (c * DB + m) * 3
                        nc.scalar.activation(d, b[:, :], ACT.Abs).then_inc(softplus_step, 1)
                        act.wait_ge(softplus_step, done + 1)
                        nc.scalar.activation(d, d, ACT.Exp, scale=-1.0).then_inc(softplus_step, 1)
                        act.wait_ge(softplus_step, done + 2)
                        nc.scalar.activation(d, d, ACT.Ln, bias=1.0).then_inc(softplus_step, 1)

            def silu_front(c, par):
                nc.scalar.preload_act_table_set(SILU_SET)
                act.wait_ge(conv_raw, (c + 1) * DB)
                nc.scalar.activation(u[:, par, :, :], u[:, par, :, :], ACT.Silu).then_inc(u_ready, 1)
                act.wait_ge(res_raw, (c + 1) * DB)
                nc.scalar.activation(z[:, par, :, :], z[:, par, :, :], ACT.Silu).then_inc(z_ready, 1)
                nc.scalar.preload_act_table_set(EXP_SET)

            def reciprocal_std(c, which):
                if which:
                    act.wait_ge(x1_ready, TT * (c + 1))
                elif isinstance(c, int):
                    after(act, o_ready, TT * c)
                act.wait_ge(stats_ready, 2 * c + which + 1)
                nc.scalar.activation(rstd[:, :], sq[:, :], ACT.Ln, bias=eps_s[:, 0:1], scale=1.0 / DM).then_inc(rstd_step, 1)
                act.wait_ge(rstd_step, 2 * (2 * c + which) + 1)
                nc.scalar.activation(rstd[:, :], rstd[:, :], ACT.Exp, scale=-0.5).then_inc(rstd_step, 1)

            def normalise(c, par, which, done):
                act.wait_ge(nmr_ready, 2 * c + which + 1)
                for t in range(TT):
                    nc.scalar.activation(xr[:, par, t, :], xr[:, par, t, :], ACT.Identity, bias=nmr[:, t:t + 1],
                                         scale=rstd[:, t:t + 1]).then_inc(done, 1)

            def back(c, par, beat):
                for name in fills(BACK_AT, beat - 1):
                    n = int(name[-1])
                    b = kp[K_AT[name] % 2]
                    if name[:3] == "x1t":
                        act.wait_ge(kp_ready, c * NK + K_AT[name] + 1)
                        copy(x1t[:, n, :], b[:, :]).then_inc(x1t_ready, 1)
                    elif name[:4] == "gate":
                        act.wait_ge(kp_ready, c * NK + K_AT[name] + 1)
                        copy(kb[:, n, :], b[:, :]).then_inc(gate_raw, 1)
                for which, (rstd_at, norm_at, done) in enumerate(((RSTD1, NORM1, x1_ready), (RSTD2, NORM2, o_ready))):
                    if beat == rstd_at:
                        reciprocal_std(c, which)
                    if beat == norm_at:
                        normalise(c, par, which, done)

            def silu_back(c):
                nc.scalar.preload_act_table_set(SILU_SET)
                act.wait_ge(gate_raw, (c + 1) * HB)
                nc.scalar.activation(kb[:, :, :], kb[:, :, :], ACT.Silu).then_inc(gate_ready, 1)
                nc.scalar.preload_act_table_set(EXP_SET)

            def exp(i, par, beat):
                n, m = beat // DB, beat % DB
                if n == 0:
                    act.wait_ge(delta_ready, i * DB + m + 1)
                slot = ahead(beat)
                if slot is None:
                    dst = da[beat % 2]
                    used = beat - 2 if ahead(beat - 2) is None else beat - 2 - AHEAD
                else:
                    dst = da_ahead[:, slot, :]
                    used = SILU_FRONT + 1 + slot if beat > SILU_BACK else SILU_BACK + 1 + slot - NH
                after(act, h_ready, i * NH + used + 1)
                nc.scalar.activation(dst[:, :], delta[:, par, m, :], ACT.Exp, scale=a_s[:, m, n:n + 1])\
                    .then_inc(da_ready, 1)

            nc.scalar.preload_act_table_set(EXP_SET)
            act.wait_ge(w_loaded, 16 * 11)
            nc.scalar.activation(a_s[:, :, :], a_s[:, :, :], ACT.Exp).then_inc(a_exp, 1)
            act.wait_ge(conv_loaded, 32)
            act.wait_ge(tiles_set, 5)
            for beat in range(NH):
                front(0, 0, beat, None)
                if beat == SILU_FRONT:
                    silu_front(0, 0)
            act.wait_ge(a_ready, 1)

            def step(i, par, j):
                first, last = [isinstance(i, int) and i == c for c in (0, NCH - 1)]
                for beat in range(NH):
                    if ahead(beat) is None:
                        exp(i, par, beat)
                    if not first:
                        back(i - 1, 1 - par, beat)
                    if not last:
                        front(i + 1, 1 - par, beat, j)
                    if beat in (SILU_FRONT, SILU_BACK):
                        for b in range(beat + 1, beat + 1 + AHEAD):
                            exp(i, par, b)
                    if beat == SILU_FRONT and not last:
                        silu_front(i + 1, 1 - par)
                    if beat == SILU_BACK and not first:
                        silu_back(i - 1)

            steps(act, step)
            for beat in range(NH):
                back(NCH - 1, (NCH - 1) % 2, beat)
                if beat == SILU_BACK:
                    silu_back(NCH - 1)

        @block.gpsimd
        def _(pool):
            nc.gpsimd.memset(ident[:, :], 0.0).then_inc(ident_zero, 1)
            pool.wait_ge(ident_zero, 1)
            nc.gpsimd.affine_select(out=ident[:, :], in_=ident[:, :], compare_op=ALU.not_equal, fill=1.0, base=0,
                                    pattern=[[-1, P]], channel_multiplier=1).then_inc(ident_ready, 1)

            def times_u(c, par, m):
                if m == 0:
                    pool.wait_ge(u_ready, c + 1)
                pool.wait_ge(delta_ready, c * DB + m + 1)
                nc.gpsimd.tensor_tensor(du[:, par, m, :], delta[:, par, m, :], u[:, par, m, :], ALU.mult)\
                    .then_inc(du_ready, 1)

            def gate_y(c, par, m):
                if m == 0:
                    pool.wait_ge(z_ready, c + 1)
                pool.wait_ge(skip_done, c * DB + m + 1)
                nc.gpsimd.tensor_tensor(kb[:, m, :], kb[:, m, :], z[:, par, m, :], ALU.mult).then_inc(y_ready, 1)

            def times_b(i, par, beat):
                n, m = beat // DB, beat % DB
                if n == 0:
                    pool.wait_ge(du_ready, i * DB + m + 1)
                if n % PIECE == 0 and m == 0:
                    piece = n // PIECE
                    pool.wait_ge(b_loaded[piece % 2], 8 * NB * i + 16 * (piece // 2 + 1))
                after(pool, h_ready, i * NH + beat + 1 - DBU)
                nc.gpsimd.tensor_tensor(dbu[:, beat % DBU, :], du[:, par, m, :],
                                        brep[:, n // PIECE % 2, n % PIECE, :], ALU.mult).then_inc(dbu_ready, 1)

            for m in range(DB):
                times_u(0, 0, m)

            def step(i, par, j):
                first, last = [isinstance(i, int) and i == c for c in (0, NCH - 1)]
                for beat in range(NH):
                    times_b(i, par, beat)
                    if not first and GATE_Y <= beat < GATE_Y + DB:
                        gate_y(i - 1, 1 - par, beat - GATE_Y)
                    if not last and TIMES_U <= beat < TIMES_U + DB:
                        times_u(i + 1, 1 - par, beat - TIMES_U)

            steps(pool, step)
            for m in range(DB):
                gate_y(NCH - 1, (NCH - 1) % 2, m)

        @block.vector
        def _(dve):
            def front(c, par, beat):
                for name in fills(FRONT_AT, beat - 1):
                    if name[:2] == "dt" and name != "dtb":
                        n, m = F_AT[name], int(name[-1])
                        dve.wait_ge(fp_ready, c * NF + n + 1)
                        dve.wait_ge(softplus_step, (c * DB + m + 1) * 3)
                        d = delta[:, par, m, :]
                        nc.vector.scalar_tensor_tensor(out=d, in0=fp[n % 2][:, :], scalar=0.0, in1=d, op0=ALU.max,
                                                       op1=ALU.add).then_inc(delta_ready, 1)

            def residual(c, par, name, done):
                n, t = K_AT[name], int(name[-1])
                dve.wait_ge(kp_ready, c * NK + n + 1)
                nc.vector.tensor_tensor(xr[:, par, t, :], kp[n % 2][:, 0:DM], xr[:, par, t, :], ALU.add)\
                    .then_inc(done, 1)

            def statistics(c, par, which, done):
                if which:
                    dve.wait_ge(nmr_ready, 2 * c + 1)
                for t in range(TT):
                    dve.wait_ge(done, c * TT + t + 1)
                    nc.vector.bn_stats(bn[:, t, :], xr[:, par, t, :]).then_inc(bn_done, 1)
                base = 4 * (2 * c + which)
                dve.wait_ge(bn_done, base + TT)
                nc.vector.tensor_tensor(mean_gap[:, :], bn[:, :, 1], bn[:, :, 4], ALU.subtract).then_inc(stats_step, 1)
                nc.vector.tensor_tensor(mean2[:, :], bn[:, :, 1], bn[:, :, 4], ALU.add).then_inc(stats_step, 1)
                nc.vector.tensor_tensor(sq[:, :], bn[:, :, 2], bn[:, :, 5], ALU.add).then_inc(stats_step, 1)
                dve.wait_ge(stats_step, base + 1)
                nc.vector.scalar_tensor_tensor(out=mean_gap[:, :], in0=mean_gap[:, :], scalar=DM / 4.0,
                                               in1=mean_gap[:, :], op0=ALU.mult, op1=ALU.mult).then_inc(stats_step, 1)
                dve.wait_ge(stats_step, base + 4)
                nc.vector.tensor_tensor(sq[:, :], sq[:, :], mean_gap[:, :], ALU.add).then_inc(stats_ready, 1)

            def shift(c, which):
                dve.wait_ge(rstd_step, 2 * (2 * c + which + 1))
                nc.vector.scalar_tensor_tensor(out=nmr[:, :], in0=mean2[:, :], scalar=-0.5, in1=rstd[:, :],
                                               op0=ALU.mult, op1=ALU.mult).then_inc(nmr_ready, 1)

            def back(c, par, beat):
                for name in fills(BACK_AT, beat - 1):
                    n, m = K_AT[name], int(name[-1])
                    if name[:2] == "yt":
                        dve.wait_ge(kp_ready, c * NK + n + 1)
                        nc.vector.scalar_tensor_tensor(out=kb[:, m, :], in0=u[:, par, m, :], scalar=d_s[:, m:m + 1],
                                                       in1=kp[n % 2][:, :], op0=ALU.mult, op1=ALU.add)\
                            .then_inc(skip_done, 1)
                    elif name[:2] == "up":
                        dve.wait_ge(gate_ready, c + 1)
                        dve.wait_ge(kp_ready, c * NK + n + 1)
                        nc.vector.tensor_tensor(kb[:, m, :], kp[n % 2][:, :], kb[:, m, :], ALU.mult)\
                            .then_inc(hid_ready, 1)
                    elif name[0] == "o":
                        if m == 0:
                            dve.wait_ge(xr_loaded[par], 8 * (c - par) + 16)
                        residual(c, par, name, res1_done)
                    elif name[:4] == "down":
                        residual(c, par, name, res2_done)
                if beat == STATS1:
                    statistics(c, par, 0, res1_done)
                if beat == SHIFT1:
                    shift(c, 0)
                if beat == STATS2:
                    statistics(c, par, 1, res2_done)
                if beat == SHIFT2:
                    shift(c, 1)

            def scan(i, beat):
                n, m = beat // DB, beat % DB
                slot = ahead(beat)
                dve.wait_ge(da_ready, i * NH + beat + 1)
                dve.wait_ge(dbu_ready, i * NH + beat + 1)
                after(dve, ht_ready, i * NHT + (n - 1) * TT)
                after(dve, carry_saved, i * NS + n - 1)
                nc.vector.tensor_tensor_scan(h[:, n % 2, m, :], da[beat % 2][:, :] if slot is None
                                             else da_ahead[:, slot, :], dbu[:, beat % DBU, :],
                                             carry[:, 1, n, m:m + 1], ALU.mult, ALU.add).then_inc(h_ready, 1)

            def save_carry(i, n):
                dve.wait_ge(h_ready, i * NH + (n + 1) * DB)
                nc.vector.tensor_copy(carry[:, 1, n, :], h[:, n % 2, :, T - 1]).then_inc(carry_saved, 1)

            def sum_states(i, par, q):
                n, t = q // TT, q % TT
                g = i * NHT + q
                dve.wait_ge(ht_ready, g + 1)
                c_col = ct[:, par, t, n:n + 1]
                if n == 0:
                    dve.wait_ge(ct_ready, i + 1)
                    ins = nc.vector.tensor_scalar(acc[:, par, t, :], ht[q % 2][:, :], c_col, None, ALU.mult)
                else:
                    dve.wait_ge(acc_done, g + 1 - TT)
                    ins = nc.vector.scalar_tensor_tensor(out=acc[:, par, t, :], in0=ht[q % 2][:, :], scalar=c_col,
                                                         in1=acc[:, par, t, :], op0=ALU.mult, op1=ALU.add)
                ins.then_inc(acc_done, 1)

            nc.vector.memset(carry[:, :, :, :], 0.0).then_inc(tiles_set, 1)
            nc.vector.memset(xin[:, :, T:T + 2 * HALO], 0.0).then_inc(tiles_set, 1)
            nc.vector.memset(xd[0:32, :], 1.0).then_inc(tiles_set, 1)
            nc.vector.memset(wx_s[:, :, R:32], 0.0).then_inc(tiles_set, 1)
            nc.vector.memset(eps_s[:, :], LN_EPS).then_inc(tiles_set, 1)
            dve.wait_ge(tiles_set, 5)
            dve.wait_ge(ident_ready, 1)
            dve.wait_ge(conv_loaded, 32)
            for m in range(DB):
                for k in range(KCONV):
                    nc.vector.tensor_scalar(diag[:, m, k, :], ident[:, :], convw_s[:, m, k:k + 1], None, ALU.mult)\
                        .then_inc(diag_ready, 1)
            dve.wait_ge(w_loaded, 16 * 11)
            for w in (wg_s, wu_s, wd_s):
                nc.vector.tensor_scalar(w[:, :, :], w[:, :, :].bitcast(I32), W_SCALE, None, ALU.mult)\
                    .then_inc(w_ready, 1)
            dve.wait_ge(a_exp, 1)
            nc.vector.tensor_scalar(a_s[:, :, :], a_s[:, :, :], -1.0, None, ALU.mult).then_inc(a_ready, 1)
            for beat in range(NH):
                front(0, 0, beat)

            def step(i, par, j):
                first = isinstance(i, int) and i == 0
                if not first:
                    save_carry(i - 1, NS - 1)
                if j is not None and par == 0:
                    dve.wait_ge(carry_saved, i * NS)
                    nc.vector.tensor_copy(carry[:, 1, :, :], carry[:, bass.ds((j + 1) % 2, 1), :, :])\
                        .then_inc(carry_reset, 1)
                    dve.wait_ge(carry_reset, j + 1)
                for beat in range(NH):
                    scan(i, beat)
                    if beat >= DB and beat % DB == 1:
                        save_carry(i, beat // DB - 1)
                    if beat > DB:
                        sum_states(i, par, beat - DB - 1)
                    elif not first:
                        sum_states(i - 1, 1 - par, NHT - DB - 1 + beat)
                    if not first:
                        back(i - 1, 1 - par, beat)
                    if not isinstance(i, int) or i < NCH - 1:
                        front(i + 1, 1 - par, beat)

            steps(dve, step)
            for q in range(NHT - DB - 1, NHT):
                sum_states(NCH - 1, (NCH - 1) % 2, q)
            for beat in range(NH):
                back(NCH - 1, (NCH - 1) % 2, beat)


def kernel(L0_attn_x, L0_attn_W_in, L0_attn_conv_w, L0_attn_conv_b, L0_attn_W_x, L0_attn_W_dt, L0_attn_b_dt,
           L0_attn_A_log, L0_attn_D, L0_attn_W_out, L0_ffn_w_gate, L0_ffn_w_up, L0_ffn_w_down):
    import numpy as np
    import concourse.bacc as bacc
    from concourse import mybir as mb
    from concourse.bass_utils import run_bass_kernel_spmd

    x = np.ascontiguousarray(L0_attn_x)
    rows = x.reshape(-1, x.shape[-1])
    arrays = {
        "x": rows, "x_t": np.ascontiguousarray(rows.T),
        "w_in": L0_attn_W_in, "conv_w": L0_attn_conv_w, "conv_b": np.asarray(L0_attn_conv_b).reshape(-1, P).T, "w_x": L0_attn_W_x,
        "w_dt": L0_attn_W_dt, "b_dt": L0_attn_b_dt, "a_log": L0_attn_A_log, "d_skip": np.asarray(L0_attn_D).reshape(-1, P).T,
        "w_out": L0_attn_W_out,
        "w_gate_t": np.asarray(L0_ffn_w_gate).T, "w_up_t": np.asarray(L0_ffn_w_up).T,
        "w_down_t": np.asarray(L0_ffn_w_down).T,
    }
    arrays = {name: np.ascontiguousarray(a) for name, a in arrays.items()}
    nc = bacc.Bacc("TRN2", target_bir_lowering=False, num_devices=1)
    args = [nc.dram_tensor(name, a.shape, mb.dt.from_np(a.dtype), kind="ExternalInput").ap()
            for name, a in arrays.items()]
    out = nc.dram_tensor("out", rows.shape, mb.dt.from_np(rows.dtype), kind="ExternalOutput").ap()
    mamba_swiglu(nc, *args, out)
    result = run_bass_kernel_spmd(nc, [arrays], core_ids=[0])
    return result.results[0]["out"].reshape(x.shape)
```

```python
from contextlib import ExitStack

import numpy as np

import concourse.bass as bass
from concourse import mybir

F32 = mybir.dt.float32
F32R = mybir.dt.float32r
F16 = mybir.dt.float16
I32 = mybir.dt.int32
ALU = mybir.AluOpType
ACT = mybir.ActivationFunctionType

P = 128
T = 512
TT = T // P
KCONV = 4
HALO = KCONV - 1
LN_EPS = 1e-5
W_SCALE = 1.0 / 127.0
EXP_SET = "natural_log_exp_and_others"
SILU_SET = "silu_and_others"

FILL_AT = {"xin0": (-1, -1), "xin1": (0, 0), "xin2": (2, 3), "yt0": (4,), "yt1": (5,), "yt2": (5,), "conv0": (7,),
           "xin3": (8, 9), "yt3": (8,), "conv1": (11,), "o0": (13, 13, 14, 14), "o1": (14, 14, 14, 14),
           "o2": (16, 16, 16, 16), "o3": (16, 16, 17, 17), "conv2": (17,), "res0": (19, 19), "conv3": (21,),
           "res1": (24, 25), "res2": (25, 25), "x1t0": (29,), "x1t1": (30,), "res3": (31, 31), "gate0": (32, 32),
           "gate1": (32, 32), "gate2": (33, 33), "gate3": (33, 33), "gate4": (34, 34), "gate5": (35, 35),
           "up0": (38, 39), "dtb": (39, 39, 40, 40), "up1": (40, 40), "up2": (42, 43), "dt0": (43,), "dt1": (43,),
           "ct": (44,), "up3": (45, 45), "up4": (45, 45), "up5": (46, 46), "dt2": (47,),
           "down0": (49, 49, 49, 50, 50, 50), "down1": (51, 51, 51, 51, 52, 52), "dt3": (56,),
           "down2": (56, 56, 57, 57, 57, 57), "down3": (59, 59, 60, 60, 60, 60)}
FILLS = list(FILL_AT)
FRONT = ("xin", "conv", "res", "dtb", "ct", "dt")
F_FILLS = [name for name in FILLS if name.rstrip("0123456789") in FRONT]
K_FILLS = [name for name in FILLS if name not in F_FILLS]
NF, NK = len(F_FILLS), len(K_FILLS)
F_AT = {name: n for n, name in enumerate(F_FILLS)}
K_AT = {name: n for n, name in enumerate(K_FILLS)}
FILL_BANKS, HT_BANKS = 3, 3
TURN_AT = (0, 0, 1, 2)

READ_AT = {"xin0": 2, "xin1": 4, "xin2": 6, "yt0": 7, "yt1": 7, "yt2": 7, "conv0": 10, "xin3": 13, "yt3": 9,
           "conv1": 16, "o0": 16, "o1": 17, "o2": 17, "o3": 18, "conv2": 22, "res0": 21, "conv3": 24, "res1": 27,
           "res2": 27, "x1t0": 32, "x1t1": 32, "res3": 32, "gate0": 33, "gate1": 34, "gate2": 36, "gate3": 37,
           "gate4": 37, "gate5": 38, "up0": 42, "dtb": 41, "up1": 42, "up2": 44, "dt0": 45, "dt1": 47, "ct": 48,
           "up3": 46, "up4": 48, "up5": 48, "dt2": 50, "down0": 54, "down1": 55, "dt3": 61, "down2": 62,
           "down3": 62}
BEAT = {"gate y": [10, 13, 13, 13], "times u": [49, 52, 55, 63], "first sum": [7, 8, 9, 10], "x1 low": [31, 31],
        "mean": [18, 62], "rstd": [20, 64], "shift": [20, 64], "norm": [23, 68], "silu u": 26, "silu gate": 39,
        "silu z": 54}
FIRST_FILLS = ["xin0", "xin1", "xin2", "xin3", "conv0", "res0", "conv1", "res1", "conv2", "res2", "conv3", "res3",
               "dtb", "dt0", "dt1", "dt2", "dt3", "ct"]
FIRST_AT = {name: n for n, name in enumerate(FIRST_FILLS)}
FIRST_BANKS = FILL_BANKS + HT_BANKS
assert sorted(FIRST_FILLS) == sorted(F_FILLS)
assert len(FIRST_FILLS) % FIRST_BANKS == 0
STORE_AT = max(BEAT["norm"][1] + 1 - 64, 0)
AHEAD = 4
SILUS = sorted(BEAT[name] for name in ("silu u", "silu z", "silu gate"))
assert all(b - a > AHEAD + 1 for a, b in zip(SILUS, SILUS[1:]))


def due(names, beat):
    return [name for name in names if READ_AT[name] == beat]


def tiles_due(kind, beat):
    return [n for n, at in enumerate(BEAT[kind]) if at == beat]


def mamba_swiglu(nc, x, x_t, w_in, conv_w, conv_b, w_x, w_dt, b_dt, a_log, d_skip, w_out, w_gate_t, w_up_t,
                 w_down_t, out):
    rows, DM = x.shape
    DI = w_out.shape[0]
    NS = a_log.shape[1]
    R = w_dt.shape[0]
    HID = w_down_t.shape[0]
    SEQ = 2048
    NCH = rows // T
    PER_SEQ = SEQ // T
    KK, DB, HB = DM // P, DI // P, HID // P
    NH = NS * DB
    NSUM = (NS - 1) * TT
    NHT = NS * TT
    PIECE = 2
    NB = NS // PIECE
    assert conv_w.shape == (P, DI // (P // KCONV))
    assert PER_SEQ == 4
    assert NH == NHT and DB == TT == 4 and KK == 2 and HB == 6 and NS == 16 and R == 16
    XB, XC = 32, 64
    XD = XC + NS
    GROUP = P // KCONV
    GROUPS = P // GROUP
    DBU = 4

    x_flat = x.rearrange("r d -> (r d)")
    out_flat = out.rearrange("r d -> (r d)")
    xt_v = x_t.rearrange("(k p) s -> p k s", p=P)
    b_rows = nc.dram_tensor("b_rows", [NS, T], F32, kind="Internal").ap()

    with ExitStack() as ctx:
        def sb(name, shape, dt=F32):
            return ctx.enter_context(nc.sbuf_tensor(name, shape, dt))

        def bank(name):
            return ctx.enter_context(nc.psum_tensor(name, [P, T], F32))

        def sem(name):
            return ctx.enter_context(nc.semaphore(name))

        win_s = sb("win_s", [P, KK, 2 * DI])
        wx_s = sb("wx_s", [P, DB, XD])
        ones_row = sb("ones_row", [XD, 1])
        wdt_s = sb("wdt_s", [R + 1, DI])
        wout_s = sb("wout_s", [P, DB, DM])
        wg_s = sb("wg_s", [P, KK, HID], F32R)
        wu_s = sb("wu_s", [P, KK, HID], F32R)
        wd_s = sb("wd_s", [P, HB, DM])
        convw_s = sb("convw_s", [P, DB, GROUPS])
        convb_s = sb("convb_s", [P, DB])
        a_s = sb("a_s", [P, DB, NS])
        d_s = sb("d_s", [P, DB])
        taps = sb("taps", [P, DB, GROUPS, GROUP])
        eye = sb("eye", [P, GROUP])
        ident = sb("ident", [P, P])
        eps_s = sb("eps_s", [P, 1])

        xt_s = sb("xt_s", [P, KK, T])
        xin = sb("xin", [P, DB, HALO + T + HALO])
        xs = sb("xs", [P, GROUPS, T])
        u = sb("u", [P, 2, DB, T])
        z = sb("z", [P, 2, DB, T])
        delta = sb("delta", [P, 2, DB, T])
        du = sb("du", [P, 2, DB, T])
        xd = sb("xd", [XD, T])
        ct = sb("ct", [P, 2, TT, NS])
        brep = sb("brep", [P, 2, PIECE, T])
        dbu = sb("dbu", [P, DBU, T])
        da_ahead = sb("da_ahead", [P, AHEAD, T])
        h = sb("h", [P, 2, DB, T])
        carry = sb("carry", [P, 2, NS, DB])
        acc = sb("acc", [P, 2, TT, DI])
        kb = sb("kb", [P, HB, T])
        xr = sb("xr", [P, 2, TT, DM])
        x1t = sb("x1t", [P, 2, KK, T], F32R)
        row_sum, neg_mean, sq = sb("row_sum", [P, 2, TT]), sb("neg_mean", [P, TT]), sb("sq", [P, TT])
        rstd = sb("rstd", [P, TT])
        nmr = sb("nmr", [P, TT])

        da = [bank(f"da{n}") for n in range(2)]
        ht = [bank(f"ht{n}") for n in range(HT_BANKS)]
        fill_banks = [bank(f"fill{n}") for n in range(FILL_BANKS)]

        win_loaded, res_loaded = sem("win_loaded"), sem("res_loaded")
        conv_loaded, w_loaded = sem("conv_loaded"), sem("w_loaded")
        small_loaded = sem("small_loaded")
        ones_set = sem("ones_set")
        ident_zero, ident_ready, tiles_set = sem("ident_zero"), sem("ident_ready"), sem("tiles_set")
        taps_ready, a_exp, a_ready, w_ready = sem("taps_ready"), sem("a_exp"), sem("a_ready"), sem("w_ready")
        da_ready, dbu_ready, h_ready = sem("da_ready"), sem("dbu_ready"), sem("h_ready")
        ht_ready, acc_begun, acc_done = sem("ht_ready"), sem("acc_begun"), sem("acc_done")
        carry_saved, carry_reset = sem("carry_saved"), sem("carry_reset")
        first_loaded = [sem(f"first_loaded{m}") for m in range(DB)]
        eye_ready, xs_loaded = sem("eye_ready"), sem("xs_loaded")
        xt_loaded, fp_ready, xin_ready = sem("xt_loaded"), sem("fp_ready"), sem("xin_ready")
        res_raw, conv_raw, u_ready, z_ready = sem("res_raw"), sem("conv_raw"), sem("u_ready"), sem("z_ready")
        xd_ready, ct_ready, softplus_step = sem("xd_ready"), sem("ct_ready"), sem("softplus_step")
        relu_ready = sem("relu_ready")
        delta_ready, du_ready, b_written = sem("delta_ready"), sem("du_ready"), sem("b_written")
        b_loaded = [sem(f"b_loaded{n}") for n in range(2)]
        xr_loaded = [sem(f"xr_loaded{n}") for n in range(2)]
        kp_ready, skip_done = sem("kp_ready"), sem("skip_done")
        y_ready, res1_done = sem("y_ready"), sem("res1_done")
        high_cut, high_ready, low_ready = sem("high_cut"), sem("high_ready"), sem("low_ready")
        gate_raw, gate_ready, hid_ready = sem("gate_raw"), sem("gate_ready"), sem("hid_ready")
        res2_done, mean_ready, sq_done = sem("res2_done"), sem("mean_ready"), sem("sq_done")
        rstd_step, nmr_ready, x1_ready = sem("rstd_step"), sem("nmr_ready"), sem("x1_ready")
        o_ready, out_stored = sem("o_ready"), sem("out_stored")

        block = ctx.enter_context(nc.Block())

        def integers(n):
            return acc[:, n, :, :].rearrange("p t d -> p (t d)")[:, 0:KK * HID].rearrange("p (k n) -> p k n", k=KK)

        def high16(k):
            return kb[:, HB - KK + k, :].bitcast(F16)[:, 0:T]

        squares = kb[:, HB - 1, :].bitcast(mybir.dt.bfloat16).rearrange("p (t d) -> p t d", t=TT)

        def xt_place(c):
            return kb[:, 0:KK, :] if isinstance(c, int) and c == 1 else xt_s[:, :, :]

        def tap_rows(c, m, rows):
            if isinstance(c, int) and c == 0 and m:
                return (h[rows, 0, :, :], h[rows, 1, :, :], da_ahead[rows, :, :])[m - 1]
            return xs[rows, :, :]

        def after(eng, semaphore, value):
            if not isinstance(value, int) or value > 0:
                eng.wait_ge(semaphore, value)

        def fill_bank(name):
            return fill_banks[FILLS.index(name) % FILL_BANKS]

        def front_bank(c, name):
            if isinstance(c, int) and c == 0:
                return (fill_banks + ht)[FIRST_AT[name] % FIRST_BANKS]
            return fill_bank(name)

        def front_filled(c, name):
            if isinstance(c, int) and c == 0:
                return FIRST_AT[name] + 1
            return c * NF + (F_AT[name] + 1)

        def ahead(beat):
            for start in SILUS:
                if start < beat <= start + AHEAD:
                    return beat - start - 1
            return None

        def times_u(eng, unit, c, par, m):
            if m == 0:
                eng.wait_ge(u_ready, c + 1)
            d = delta[:, par, m, :]
            eng.wait_ge(relu_ready, c * DB + m + 1)
            eng.wait_ge(softplus_step, (c * DB + m + 1) * 3)
            unit.tensor_tensor(d, d, du[:, par, m, :], ALU.add).then_inc(delta_ready, 1)
            eng.wait_ge(delta_ready, c * DB + m + 1)
            unit.tensor_tensor(du[:, par, m, :], d, u[:, par, m, :], ALU.mult).then_inc(du_ready, 1)

        def steps(eng, step):
            step(0, 0, None)
            step(1, 1, None)
            with eng.Fori(0, (NCH - 4) // 2) as j:
                step(2 * j + 2, 0, j)
                step(2 * j + 3, 1, j)
            step(NCH - 2, 0, None)
            step(NCH - 1, 1, None)

        @block.sync
        def _(sp):
            def load_xt(c):
                sp.dma_start(xt_place(c), xt_v[:, :, bass.ds(c * T, T)]).then_inc(xt_loaded, 16)

            def tokens(flat, start):
                return flat[bass.ds(start, T * DM)].rearrange("(t p d) -> p t d", p=P, t=TT)

            def load_x(c, par):
                sp.dma_start(xr[:, par, :, :], tokens(x_flat, c * (T * DM))).then_inc(xr_loaded[par], 16)

            def store(c, par):
                sp.wait_ge(o_ready, TT * (c + 1))
                sp.dma_start(tokens(out_flat, c * (T * DM)), xr[:, par, :, :]).then_inc(out_stored, 16)

            def shift_xin(c, m):
                if m == 0 or isinstance(c, int) and c == 0:
                    sp.wait_ge(xin_ready, c * (DB + 1) + (m + 2))
                else:
                    sp.wait_ge(fp_ready, c * NF + (F_AT[f"conv{m - 1}"] + 1))
                for k in range(KCONV):
                    sp.dma_start(tap_rows(c, m, slice(k * GROUP, (k + 1) * GROUP)), xin[:, m, k:k + T])\
                        .then_inc(first_loaded[m] if isinstance(c, int) and c == 0 else xs_loaded, 16)

            def write_b(c):
                for half in range(2):
                    after(sp, b_loaded[half], 8 * NB * c)
                after(sp, xd_ready, 2 * c + 2)
                sp.dma_start(b_rows, xd[XB:XB + NS, :]).then_inc(b_written, 16)

            def spread_b(c, p, later=0):
                if p == 0:
                    after(sp, b_written, c * 16 + 16 * (later + 1))
                    if later:
                        after(sp, dbu_ready, (c * 8 + (NB - 1)) * (NH // 8))
                else:
                    after(sp, dbu_ready, c * NH + (later * NH + (p - 1) * PIECE * DB))
                sp.dma_start(brep[:, p % 2, :, :],
                             b_rows[p * PIECE:(p + 1) * PIECE, :].partition_broadcast(P))\
                    .then_inc(b_loaded[p % 2], 16)

            load_xt(0)
            w_in_v = w_in.rearrange("(k p) n -> p k n", p=P)
            sp.dma_start(win_s[:, :, 0:DI], w_in_v[:, :, 0:DI]).then_inc(win_loaded, 16)
            sp.dma_start(convw_s[:, :, :], conv_w.rearrange("p (m g) -> p m g", m=DB)).then_inc(conv_loaded, 16)
            sp.dma_start(convb_s[:, :], conv_b).then_inc(conv_loaded, 16)
            sp.dma_start(win_s[:, :, DI:2 * DI], w_in_v[:, :, DI:2 * DI]).then_inc(res_loaded, 16)
            w_x_v = w_x.rearrange("(m p) n -> p m n", p=P)
            sp.dma_start(wx_s[:, :, 0:R], w_x_v[:, :, 0:R]).then_inc(small_loaded, 16)
            sp.dma_start(wx_s[:, :, XB:XB + NS], w_x_v[:, :, R:R + NS]).then_inc(small_loaded, 16)
            sp.dma_start(wx_s[:, :, XC:XC + NS], w_x_v[:, :, R + NS:R + 2 * NS]).then_inc(small_loaded, 16)
            sp.dma_start(wdt_s[0:R, :], w_dt).then_inc(small_loaded, 16)
            sp.dma_start(wdt_s[R:R + 1, :], b_dt.rearrange("(a n) -> a n", a=1)).then_inc(small_loaded, 16)
            sp.dma_start(a_s[:, :, :], a_log.rearrange("(m p) n -> p m n", p=P)).then_inc(small_loaded, 16)
            sp.dma_start(d_s[:, :], d_skip).then_inc(small_loaded, 16)
            for m in range(DB):
                shift_xin(0, m)
            sp.dma_start(wout_s[:, :, :], w_out.rearrange("(m p) n -> p m n", p=P)).then_inc(w_loaded, 16)
            for tile, w in ((integers(0), w_gate_t), (integers(1), w_up_t), (wd_s[:, :, :], w_down_t)):
                sp.dma_start(tile.bitcast(I32), w.rearrange("(k p) n -> p k n", p=P)).then_inc(w_loaded, 16)
            load_xt(1)
            load_x(0, 0)
            load_x(1, 1)
            write_b(0)
            spread_b(0, 0)
            spread_b(0, 1)

            SP_ORDER = [kind for _, kind in sorted(
                [(PIECE * DB * (p - 1), ("b", p)) for p in range(2, NB)]
                + [(NH - PIECE * DB + PIECE * DB * p, ("next b", p)) for p in range(2)]
                + [(max(READ_AT[f"xin{m}"] - 1, FILL_AT[f"conv{m - 1}"][-1] + 1 if m else 0), ("xin", m))
                   for m in range(DB)]
                + [(STORE_AT, ("store", 0)), (STORE_AT + 6, ("load x", 0))]
                + [(max(FILL_AT["xin3"][-1], FILL_AT["res3"][-1]) + 1, ("xt", 0)),
                   (max(READ_AT["dtb"], PIECE * DB * (NB - 2) + 1), ("write b", 0))])]

            def step(i, par, j):
                first, last = [isinstance(i, int) and i == c for c in (0, NCH - 1)]
                for kind, n in SP_ORDER:
                    if kind == "b":
                        spread_b(i, n)
                    elif kind == "next b" and not last:
                        spread_b(i, n, 1)
                    elif kind == "xin" and not last:
                        shift_xin(i + 1, n)
                    elif kind == "write b" and not last:
                        write_b(i + 1)
                    elif kind == "store" and not (isinstance(i, int) and i < 2):
                        store(i - 2, par)
                    elif kind == "load x" and not (isinstance(i, int) and i < 2):
                        sp.wait_ge(out_stored, 16 * (i - 1))
                        load_x(i, par)
                    elif kind == "xt" and not (isinstance(i, int) and i + 2 >= NCH):
                        after(sp, fp_ready, (i + 1) * NF + max(F_AT[name] for name in ("xin3", "res3")) + 1)
                        load_xt(i + 2)

            steps(sp, step)
            store(NCH - 2, NCH % 2)
            for t in range(TT):
                sp.wait_ge(o_ready, TT * (NCH - 1) + t + 1)
                sp.dma_start(out[(NCH - 1) * T + t * P:(NCH - 1) * T + (t + 1) * P, :], xr[:, (NCH - 1) % 2, t, :])\
                    .then_inc(out_stored, 16)
            sp.wait_ge(xt_loaded, 16 * NCH)
            sp.wait_ge(out_stored, 16 * (NCH - 1) + 16 * TT)
            sp.wait_ge(b_written, 16 * NCH)

        @block.tensor
        def _(pe):
            taken = {}
            for m in range(4):
                taken[f"xin{m}"] = (xin_ready, DB + 1, m + 2)
                taken[f"conv{m}"] = (conv_raw, DB, m + 1)
                taken[f"res{m}"] = (res_raw, DB, m + 1)
                taken[f"dt{m}"] = (softplus_step, 3 * DB, 3 * m + 1)
                taken[f"yt{m}"] = (skip_done, DB, m + 1)
                taken[f"o{m}"] = (res1_done, TT, m + 1)
                taken[f"down{m}"] = (res2_done, TT, TT + m + 1)
            taken["dtb"] = (xd_ready, 2, 2)
            taken["ct"] = (ct_ready, 1, 1)
            for k in range(KK):
                taken[f"x1t{k}"] = (low_ready, KK, k + 1)
            for m in range(HB):
                taken[f"gate{m}"] = (gate_raw, HB, m + 1)
                taken[f"up{m}"] = (hid_ready, HB, m + 1)

            def wait_bank(i, name):
                if isinstance(i, int) and i == -1:
                    if FIRST_AT[name] >= FIRST_BANKS:
                        s, _, count = taken[FIRST_FILLS[FIRST_AT[name] - FIRST_BANKS]]
                        pe.wait_ge(s, count)
                    return
                n, back_by, seen = FILLS.index(name), 0, False
                while True:
                    n -= FILL_BANKS
                    if n < 0:
                        n = max(k for k in range(len(FILLS)) if (k - n) % FILL_BANKS == 0)
                        back_by += 1
                        if isinstance(i, int) and i - back_by < -1:
                            return
                    front = FILLS[n] in F_FILLS
                    later = (1 if front else -1) - back_by
                    if isinstance(i, int) and not 0 <= i + later < NCH or not front and seen:
                        continue
                    s, per, count = taken[FILLS[n]]
                    pe.wait_ge(s, i * per + (later * per + count))
                    if front or not back_by:
                        return
                    seen = True

            def in_proj(c, name, m, k):
                if k == 0:
                    pe.wait_ge(xt_loaded, 16 * (c + 1))
                    wait_bank(c - 1, name)
                mm = nc.tensor.matmul(front_bank(c, name)[:, :], win_s[:, k, m * P:(m + 1) * P], xt_place(c)[:, k, :],
                                      start=(k == 0), stop=(k == KK - 1))
                if k == KK - 1:
                    mm.then_inc(fp_ready, 1)

            def conv(c, name, m):
                if isinstance(c, int) and c == 0:
                    pe.wait_ge(first_loaded[m], 16 * KCONV)
                else:
                    if m + 1 < DB:
                        pe.wait_ge(xin_ready, c * (DB + 1) + (m + 3))
                    pe.wait_ge(xs_loaded, 16 * KCONV * DB * (c - 1) + 16 * KCONV * (m + 1))
                wait_bank(c - 1, name)
                for g in range(GROUPS):
                    mm = nc.tensor.matmul(front_bank(c, name)[g * GROUP:(g + 1) * GROUP, :], taps[:, m, g, :],
                                          tap_rows(c, m, slice(0, P))[:, g, :], start=True, stop=True)
                mm.then_inc(fp_ready, 1)

            def dt_b(c, par, m):
                if m == 0:
                    pe.wait_ge(u_ready, c + 1)
                    wait_bank(c - 1, "dtb")
                mm = nc.tensor.matmul(front_bank(c, "dtb")[0:XD, :], wx_s[:, m, :], u[:, par, m, :],
                                      start=(m == 0), stop=(m == DB - 1))
                if m == DB - 1:
                    mm.then_inc(fp_ready, 1)

            def turn_c(c):
                pe.wait_ge(xd_ready, 2 * c + 2)
                wait_bank(c - 1, "ct")
                for t in range(TT):
                    mm = nc.tensor.matmul(front_bank(c, "ct")[:, t * NS:(t + 1) * NS], xd[XC:XC + NS, t * P:(t + 1) * P],
                                          ident[XC:XC + NS, XC:XC + NS], start=True, stop=True)
                mm.then_inc(fp_ready, 1)

            def dt_proj(c, name, m):
                pe.wait_ge(xd_ready, 2 * c + 2)
                wait_bank(c - 1, name)
                nc.tensor.matmul(front_bank(c, name)[:, :], wdt_s[:, m * P:(m + 1) * P], xd[0:R + 1, :],
                                 start=True, stop=True).then_inc(fp_ready, 1)

            def turn_sum(c, name, par, m):
                pe.wait_ge(acc_done, (c + 1) * NSUM)
                wait_bank(c + 1, name)
                for t in range(TT):
                    mm = nc.tensor.transpose(fill_bank(name)[:, t * P:(t + 1) * P],
                                             acc[:, par, t, m * P:(m + 1) * P], ident[:, :])
                mm.then_inc(kp_ready, 1)

            def out_proj(c, name, t, m):
                if m == 0:
                    pe.wait_ge(y_ready, (c + 1) * DB)
                    wait_bank(c + 1, name)
                mm = nc.tensor.matmul(fill_bank(name)[:, 0:DM], kb[:, m, t * P:(t + 1) * P], wout_s[:, m, :],
                                      start=(m == 0), stop=(m == DB - 1))
                if m == DB - 1:
                    mm.then_inc(kp_ready, 1)

            def turn_x1(c, name, par, k):
                pe.wait_ge(x1_ready, (c + 1) * TT)
                wait_bank(c + 1, name)
                for t in range(TT):
                    mm = nc.tensor.transpose(fill_bank(name)[:, t * P:(t + 1) * P],
                                             xr[:, par, t, k * P:(k + 1) * P], ident[:, :])
                mm.then_inc(kp_ready, 1)

            def hidden(c, name, w, n, k):
                if k == 0:
                    pe.wait_ge(high_ready, (c + 1) * KK)
                    pe.wait_ge(low_ready, (c + 1) * KK)
                    wait_bank(c + 1, name)
                for half in range(2):
                    mm = nc.tensor.matmul(fill_bank(name)[:, :], w[:, k, n * P:(n + 1) * P], x1t[:, half, k, :],
                                          start=(k == 0 and half == 0), stop=(k == KK - 1 and half == 1))
                if k == KK - 1:
                    mm.then_inc(kp_ready, 1)

            def down(c, name, t, n):
                if n == 0:
                    pe.wait_ge(hid_ready, (c + 1) * HB)
                    wait_bank(c + 1, name)
                mm = nc.tensor.matmul(fill_bank(name)[:, 0:DM], kb[:, n, t * P:(t + 1) * P], wd_s[:, n, :],
                                      start=(n == 0), stop=(n == HB - 1))
                if n == HB - 1:
                    mm.then_inc(kp_ready, 1)

            def fill_ahead(i, beat):
                for m in range(DB):
                    for k, at in enumerate(FILL_AT[f"xin{m}"]):
                        if at == beat - NH:
                            in_proj(i + 2, f"xin{m}", m, k)

            def fill(i, par, beat, front, back):
                for name, beats in FILL_AT.items():
                    if not (front if name in F_FILLS else back):
                        continue
                    kind, n = name.rstrip("0123456789"), int(name[-1]) if name[-1].isdigit() else 0
                    for part, at in enumerate(beats):
                        if at != beat:
                            continue
                        if kind == "xin":
                            in_proj(i + 1, name, n, part)
                        elif kind == "res":
                            in_proj(i + 1, name, DB + n, part)
                        elif kind == "conv":
                            conv(i + 1, name, n)
                        elif kind == "dtb":
                            dt_b(i + 1, par, part)
                        elif kind == "ct":
                            turn_c(i + 1)
                        elif kind == "dt":
                            dt_proj(i + 1, name, n)
                        elif kind == "yt":
                            turn_sum(i - 1, name, par, n)
                        elif kind == "o":
                            out_proj(i - 1, name, n, part)
                        elif kind == "x1t":
                            turn_x1(i - 1, name, par, n)
                        elif kind == "gate":
                            hidden(i - 1, name, wg_s, n, part)
                        elif kind == "up":
                            hidden(i - 1, name, wu_s, n, part)
                        else:
                            down(i - 1, name, n, part)

            def turn(i, q):
                n, t = q // TT, q % TT
                pe.wait_ge(h_ready, i * NH + (n + 1) * DB)
                before = ht_before(q)
                if 0 <= before < TT:
                    pe.wait_ge(acc_begun, i * TT + before + 1)
                else:
                    after(pe, acc_done, i * NSUM + (before if before < 0 else before - TT) + 1)
                for m in range(DB):
                    mm = nc.tensor.transpose(ht[q % HT_BANKS][:, m * P:(m + 1) * P],
                                             h[:, n % 2, m, t * P:(t + 1) * P], ident[:, :])
                mm.then_inc(ht_ready, 1)

            def ht_before(q):
                return q - HT_BANKS if q >= HT_BANKS else max(p for p in range(NHT) if (p - q) % HT_BANKS == 0) - NHT

            def turns(i, beat):
                n = beat // TT - 1
                for t in range(TT):
                    if TURN_AT[t] == beat % TT:
                        turn(i - 1 if n < 0 else i, (NS - 1 if n < 0 else n) * TT + t)

            pe.wait_ge(win_loaded, 16)
            pe.wait_ge(ident_ready, 1)
            for m in range(DB):
                for k in range(KK):
                    in_proj(0, f"xin{m}", m, k)
            pe.wait_ge(taps_ready, DB * GROUPS)
            pe.wait_ge(res_loaded, 16)
            for m in range(DB):
                conv(0, f"conv{m}", m)
                for k in range(KK):
                    in_proj(0, f"res{m}", DB + m, k)
            pe.wait_ge(small_loaded, 16 * 7)
            pe.wait_ge(tiles_set, 5)
            for m in range(DB):
                dt_b(0, 0, m)
            for m in range(DB):
                dt_proj(0, f"dt{m}", m)
            turn_c(0)
            for n, name in enumerate(FIRST_FILLS[-FIRST_BANKS:]):
                if n == FILL_BANKS:
                    for beat in range(NH):
                        fill_ahead(-1, beat)
                s, _, count = taken[name]
                pe.wait_ge(s, count)
            pe.wait_ge(w_loaded, 16 * 4)
            pe.wait_ge(w_ready, 3)

            def step(i, par, j):
                first, last = [isinstance(i, int) and i == c for c in (0, NCH - 1)]
                for beat in range(NH):
                    if not first or beat >= DB:
                        turns(i, beat)
                    fill(i, 1 - par, beat, not last, not first)
                    if not (isinstance(i, int) and i + 2 >= NCH):
                        fill_ahead(i, beat)

            steps(pe, step)
            for beat in range(NH):
                if beat < DB:
                    turns(NCH, beat)
                fill(NCH, (NCH - 1) % 2, beat, False, True)

        @block.scalar
        def _(act):
            def copy(dst, src):
                return nc.scalar.activation(dst, src, ACT.Copy)

            def front(c, par, beat, j):
                if beat == 0:
                    start = T + HALO * ((j + 1) % 2) if j is not None and par == 0 else T
                    after(act, xin_ready, c * (DB + 1))
                    copy(xin[:, :, 0:HALO], xin[:, :, bass.ds(start, HALO)]).then_inc(xin_ready, 1)
                read_front(c, par, due(F_FILLS, beat))

            def read_front(c, par, names):
                for name in names:
                    m = int(name[-1]) if name[-1].isdigit() else 0
                    b = front_bank(c, name)
                    act.wait_ge(fp_ready, front_filled(c, name))
                    if name[:3] == "xin":
                        act.wait_ge(xin_ready, c * (DB + 1) + 1)
                        copy(xin[:, m, HALO:HALO + T], b[:, :]).then_inc(xin_ready, 1)
                    elif name[:3] == "res":
                        after(act, y_ready, (c - 2) * DB + m + 1)
                        copy(z[:, par, m, :], b[:, :]).then_inc(res_raw, 1)
                    elif name[:4] == "conv":
                        after(act, skip_done, (c - 2) * DB + m + 1)
                        nc.scalar.activation(u[:, par, m, :], b[:, :], ACT.Identity,
                                             bias=convb_s[:, m:m + 1]).then_inc(conv_raw, 1)
                    elif name == "dtb":
                        after(act, b_written, 16 * c)
                        nc.scalar.activation(xd[:, :], b[0:XD, :], ACT.Identity, bias=ones_row[:, 0:1])\
                            .then_inc(xd_ready, 2)
                    elif name == "ct":
                        copy(ct[:, par, :, :], b[:, 0:TT * NS].rearrange("p (t n) -> p t n", n=NS))\
                            .then_inc(ct_ready, 1)
                    else:
                        d = delta[:, par, m, :]
                        done = (c * DB + m) * 3
                        nc.scalar.activation(du[:, par, m, :], b[:, :], ACT.Relu).then_inc(relu_ready, 1)
                        nc.scalar.activation(d, b[:, :], ACT.Abs).then_inc(softplus_step, 1)
                        act.wait_ge(softplus_step, done + 1)
                        nc.scalar.activation(d, d, ACT.Exp, scale=-1.0).then_inc(softplus_step, 1)
                        act.wait_ge(softplus_step, done + 2)
                        nc.scalar.activation(d, d, ACT.Ln, bias=1.0).then_inc(softplus_step, 1)

            def silu_u(c, par):
                nc.scalar.preload_act_table_set(SILU_SET)
                act.wait_ge(conv_raw, (c + 1) * DB)
                nc.scalar.activation(u[:, par, :, :], u[:, par, :, :], ACT.Silu).then_inc(u_ready, 1)
                nc.scalar.preload_act_table_set(EXP_SET)

            def silu_g(c):
                nc.scalar.preload_act_table_set(SILU_SET)
                act.wait_ge(gate_raw, (c + 1) * HB)
                nc.scalar.activation(kb[:, :, :], kb[:, :, :], ACT.Silu).then_inc(gate_ready, 1)
                nc.scalar.preload_act_table_set(EXP_SET)

            def silu_z(c, par):
                nc.scalar.preload_act_table_set(SILU_SET)
                act.wait_ge(res_raw, (c + 1) * DB)
                nc.scalar.activation(z[:, par, :, :], z[:, par, :, :], ACT.Silu).then_inc(z_ready, 1)
                nc.scalar.preload_act_table_set(EXP_SET)

            def reciprocal_std(c, par, which):
                if which:
                    act.wait_ge(x1_ready, TT * (c + 1))
                elif isinstance(c, int):
                    after(act, o_ready, TT * c)
                act.wait_ge(mean_ready, 2 * c + which + 1)
                for t in range(TT):
                    nc.scalar.activation(squares[:, t, :], xr[:, par, t, :], ACT.Square, bias=neg_mean[:, t:t + 1],
                                         accum_out=sq[:, t:t + 1]).then_inc(sq_done, 1)
                act.wait_ge(sq_done, TT * (2 * c + which + 1))
                nc.scalar.activation(rstd[:, :], sq[:, :], ACT.Ln, bias=eps_s[:, 0:1], scale=1.0 / DM)\
                    .then_inc(rstd_step, 1)
                act.wait_ge(rstd_step, 2 * (2 * c + which) + 1)
                nc.scalar.activation(rstd[:, :], rstd[:, :], ACT.Exp, scale=-0.5).then_inc(rstd_step, 1)

            def normalise(c, par, which, done):
                act.wait_ge(nmr_ready, 2 * c + which + 1)
                for t in range(TT):
                    nc.scalar.activation(xr[:, par, t, :], xr[:, par, t, :], ACT.Identity, bias=nmr[:, t:t + 1],
                                         scale=rstd[:, t:t + 1]).then_inc(done, 1)

            def back(c, par, beat):
                alone = isinstance(c, int) and c == NCH - 1
                for name in due(K_FILLS, beat):
                    n = int(name[-1])
                    b = fill_bank(name)
                    if name[:3] == "x1t":
                        act.wait_ge(kp_ready, c * NK + K_AT[name] + 1)
                        copy(high16(n), b[:, :]).then_inc(high_cut, 1)
                        act.wait_ge(high_cut, c * KK + n + 1)
                        copy(x1t[:, 0, n, :], high16(n)).then_inc(high_ready, 1)
                    elif name[:4] == "gate":
                        act.wait_ge(kp_ready, c * NK + K_AT[name] + 1)
                        nc.scalar.activation(kb[:, n, :], b[:, :], ACT.Silu if alone else ACT.Copy, scale=W_SCALE)\
                            .then_inc(gate_raw, 1)
                    elif alone and (name[0] == "o" or name[:4] == "down"):
                        tile_norm(c, par, int(name[0] == "d"), n)
                if not alone:
                    norms(c, par, beat)

            def tile_norm(c, par, which, t):
                k = which * TT + t
                if which:
                    act.wait_ge(x1_ready, TT * (c + 1))
                else:
                    act.wait_ge(o_ready, TT * c)
                act.wait_ge(mean_ready, 2 * c + k + 1)
                nc.scalar.activation(h[:, which, t, 0:DM], xr[:, par, t, :], ACT.Square, bias=neg_mean[:, t:t + 1],
                                     accum_out=sq[:, t:t + 1]).then_inc(sq_done, 1)
                act.wait_ge(sq_done, TT * 2 * c + k + 1)
                nc.scalar.activation(rstd[:, t:t + 1], sq[:, t:t + 1], ACT.Ln, bias=eps_s[:, 0:1], scale=1.0 / DM)\
                    .then_inc(rstd_step, 1)
                act.wait_ge(rstd_step, 2 * (2 * c + k) + 1)
                nc.scalar.activation(rstd[:, t:t + 1], rstd[:, t:t + 1], ACT.Exp, scale=-0.5).then_inc(rstd_step, 1)
                act.wait_ge(nmr_ready, 2 * c + k + 1)
                nc.scalar.activation(xr[:, par, t, :], xr[:, par, t, :], ACT.Identity, bias=nmr[:, t:t + 1],
                                     scale=rstd[:, t:t + 1]).then_inc((x1_ready, o_ready)[which], 1)

            def norms(c, par, beat):
                for which in tiles_due("rstd", beat):
                    reciprocal_std(c, par, which)
                for which in tiles_due("norm", beat):
                    normalise(c, par, which, (x1_ready, o_ready)[which])

            def exp(i, par, beat):
                n, m = beat // DB, beat % DB
                if n == 0:
                    act.wait_ge(delta_ready, i * DB + m + 1)
                slot = ahead(beat)
                if slot is None:
                    dst, used = da[beat % 2], beat - 2
                    while ahead(used) is not None:
                        used -= 2
                else:
                    dst = da_ahead[:, slot, :]
                    window = SILUS.index(beat - slot - 1)
                    used = (SILUS[window - 1] - (0 if window else NH)) + 1 + slot
                after(act, h_ready, i * NH + used + 1)
                nc.scalar.activation(dst[:, :], delta[:, par, m, :], ACT.Exp, scale=a_s[:, m, n:n + 1])\
                    .then_inc(da_ready, 1)

            def begin_sum(i, par, q):
                act.wait_ge(ct_ready, i + 1)
                act.wait_ge(ht_ready, i * NHT + q + 1)
                nc.scalar.activation(acc[:, par, q, :], ht[q % HT_BANKS][:, :], ACT.Copy, scale=ct[:, par, q, 0:1])\
                    .then_inc(acc_begun, 1)

            nc.scalar.preload_act_table_set(SILU_SET)
            act.wait_ge(conv_loaded, 32)
            act.wait_ge(tiles_set, 5)
            copy(xin[:, :, 0:HALO], xin[:, :, T:T + HALO]).then_inc(xin_ready, 1)
            read_front(0, 0, FIRST_FILLS[:FIRST_AT["conv3"] + 1])
            act.wait_ge(conv_raw, DB)
            nc.scalar.activation(u[:, 0, :, :], u[:, 0, :, :], ACT.Silu).then_inc(u_ready, 1)
            read_front(0, 0, ["res3"])
            act.wait_ge(res_raw, DB)
            nc.scalar.activation(z[:, 0, :, :], z[:, 0, :, :], ACT.Silu).then_inc(z_ready, 1)
            nc.scalar.preload_act_table_set(EXP_SET)
            act.wait_ge(small_loaded, 16 * 7)
            nc.scalar.activation(a_s[:, :, :], a_s[:, :, :], ACT.Exp).then_inc(a_exp, 1)
            read_front(0, 0, FIRST_FILLS[FIRST_AT["res3"] + 1:])
            act.wait_ge(a_ready, 1)

            def step(i, par, j):
                first, last = [isinstance(i, int) and i == c for c in (0, NCH - 1)]
                for beat in range(NH):
                    if ahead(beat) is None:
                        exp(i, par, beat)
                    for t in tiles_due("first sum", beat):
                        begin_sum(i, par, t)
                    if not (isinstance(i, int) and i < 2):
                        norms(i - 2, par, NH + beat)
                    if not first:
                        back(i - 1, 1 - par, beat)
                    if not last:
                        front(i + 1, 1 - par, beat, j)
                    if beat in SILUS:
                        for b in range(beat + 1, beat + 1 + AHEAD):
                            exp(i, par, b)
                    if beat == BEAT["silu u"] and not last:
                        silu_u(i + 1, 1 - par)
                    if beat == BEAT["silu z"] and not last:
                        silu_z(i + 1, 1 - par)
                    if beat == BEAT["silu gate"] and not first:
                        silu_g(i - 1)

            steps(act, step)
            for beat in range(NH):
                if beat == READ_AT["gate0"]:
                    nc.scalar.preload_act_table_set(SILU_SET)
                norms(NCH - 2, NCH % 2, NH + beat)
                back(NCH - 1, (NCH - 1) % 2, beat)
                if beat == READ_AT["gate5"]:
                    nc.scalar.preload_act_table_set(EXP_SET)

        @block.gpsimd
        def _(pool):
            nc.gpsimd.memset(ident[:, :], 0.0).then_inc(ident_zero, 1)
            pool.wait_ge(ident_zero, 1)
            nc.gpsimd.affine_select(out=ident[:, :], in_=ident[:, :], compare_op=ALU.not_equal, fill=1.0, base=0,
                                    pattern=[[-1, P]], channel_multiplier=1).then_inc(ident_ready, 1)

            def gate_y(c, par, m):
                if m == 0:
                    pool.wait_ge(z_ready, c + 1)
                pool.wait_ge(skip_done, c * DB + m + 1)
                nc.gpsimd.tensor_tensor(kb[:, m, :], kb[:, m, :], z[:, par, m, :], ALU.mult).then_inc(y_ready, 1)

            def times_b(i, par, beat):
                n, m = beat // DB, beat % DB
                if n == 0:
                    pool.wait_ge(du_ready, i * DB + m + 1)
                if n % PIECE == 0 and m == 0:
                    piece = n // PIECE
                    pool.wait_ge(b_loaded[piece % 2], 8 * NB * i + 16 * (piece // 2 + 1))
                after(pool, h_ready, i * NH + beat + 1 - DBU)
                nc.gpsimd.tensor_tensor(dbu[:, beat % DBU, :], du[:, par, m, :],
                                        brep[:, n // PIECE % 2, n % PIECE, :], ALU.mult).then_inc(dbu_ready, 1)

            def step(i, par, j):
                first, last = [isinstance(i, int) and i == c for c in (0, NCH - 1)]
                for beat in range(NH):
                    times_b(i, par, beat)
                    for m in [] if first else tiles_due("gate y", beat):
                        gate_y(i - 1, 1 - par, m)
                    for m in [] if last else tiles_due("times u", beat):
                        times_u(pool, nc.gpsimd, i + 1, 1 - par, m)

            steps(pool, step)

        @block.vector
        def _(dve):
            def residual(c, par, name, which):
                n, t = K_AT[name], int(name[-1])
                dve.wait_ge(kp_ready, c * NK + n + 1)
                nc.vector.scalar_tensor_tensor(out=xr[:, par, t, :], in0=fill_bank(name)[:, 0:DM], scalar=1.0,
                                               in1=xr[:, par, t, :], op0=ALU.mult, op1=ALU.add,
                                               accum_out=row_sum[:, which, t:t + 1])\
                    .then_inc((res1_done, res2_done)[which], 1)

            def minus_mean(c, which):
                dve.wait_ge((res1_done, res2_done)[which], (c + which + 1) * TT)
                if which:
                    dve.wait_ge(nmr_ready, 2 * c + 1)
                nc.vector.tensor_scalar(neg_mean[:, :], row_sum[:, which, :], -1.0 / DM, None, ALU.mult)\
                    .then_inc(mean_ready, 1)

            def shift(c, which):
                dve.wait_ge(rstd_step, 2 * (2 * c + which + 1))
                nc.vector.scalar_tensor_tensor(out=nmr[:, :], in0=neg_mean[:, :], scalar=1.0, in1=rstd[:, :],
                                               op0=ALU.mult, op1=ALU.mult).then_inc(nmr_ready, 1)

            def back(c, par, beat):
                alone = isinstance(c, int) and c == NCH - 1
                for name in due(K_FILLS, beat):
                    n, m = K_AT[name], int(name[-1])
                    if name[:2] == "yt":
                        dve.wait_ge(kp_ready, c * NK + n + 1)
                        nc.vector.scalar_tensor_tensor(out=kb[:, m, :], in0=u[:, par, m, :], scalar=d_s[:, m:m + 1],
                                                       in1=fill_bank(name)[:, :], op0=ALU.mult, op1=ALU.add)\
                            .then_inc(skip_done, 1)
                        if alone:
                            dve.wait_ge(z_ready, c + 1)
                            dve.wait_ge(skip_done, c * DB + m + 1)
                            nc.vector.tensor_tensor(kb[:, m, :], kb[:, m, :], z[:, par, m, :], ALU.mult)\
                                .then_inc(y_ready, 1)
                    elif name[:2] == "up":
                        if alone:
                            dve.wait_ge(gate_raw, c * HB + m + 1)
                        else:
                            dve.wait_ge(gate_ready, c + 1)
                        dve.wait_ge(kp_ready, c * NK + n + 1)
                        nc.vector.scalar_tensor_tensor(out=kb[:, m, :], in0=fill_bank(name)[:, :], scalar=W_SCALE,
                                                       in1=kb[:, m, :], op0=ALU.mult, op1=ALU.mult)\
                            .then_inc(hid_ready, 1)
                    elif name[0] == "o":
                        if m == 0:
                            dve.wait_ge(xr_loaded[par], 8 * (c - par) + 16)
                        residual(c, par, name, 0)
                        if alone:
                            tile_shift(c, 0, m)
                    elif name[:4] == "down":
                        residual(c, par, name, 1)
                        if alone:
                            tile_shift(c, 1, m)
                for k in tiles_due("x1 low", beat):
                    dve.wait_ge(high_cut, c * KK + k + 1)
                    nc.vector.tensor_tensor(x1t[:, 1, k, :], fill_bank(f"x1t{k}")[:, :], high16(k), ALU.subtract)\
                        .then_inc(low_ready, 1)
                if not alone:
                    norms(c, beat)

            def tile_shift(c, which, t):
                k = which * TT + t
                dve.wait_ge((res1_done, res2_done)[which], (c + which) * TT + t + 1)
                if which:
                    dve.wait_ge(nmr_ready, 2 * c + TT)
                nc.vector.tensor_scalar(neg_mean[:, t:t + 1], row_sum[:, which, t:t + 1], -1.0 / DM, None, ALU.mult)\
                    .then_inc(mean_ready, 1)
                dve.wait_ge(rstd_step, 2 * (2 * c + k + 1))
                nc.vector.scalar_tensor_tensor(out=nmr[:, t:t + 1], in0=neg_mean[:, t:t + 1], scalar=1.0,
                                               in1=rstd[:, t:t + 1], op0=ALU.mult, op1=ALU.mult)\
                    .then_inc(nmr_ready, 1)

            def norms(c, beat):
                for which in tiles_due("mean", beat):
                    minus_mean(c, which)
                for which in tiles_due("shift", beat):
                    shift(c, which)

            def scan(i, beat):
                n, m = beat // DB, beat % DB
                slot = ahead(beat)
                dve.wait_ge(da_ready, i * NH + beat + 1)
                dve.wait_ge(dbu_ready, i * NH + beat + 1)
                after(dve, ht_ready, i * NHT + (n - 1) * TT)
                after(dve, carry_saved, i * NS + n - 1)
                nc.vector.tensor_tensor_scan(h[:, n % 2, m, :], da[beat % 2][:, :] if slot is None
                                             else da_ahead[:, slot, :], dbu[:, beat % DBU, :],
                                             carry[:, 1, n, m:m + 1], ALU.mult, ALU.add).then_inc(h_ready, 1)

            def save_carry(i, n):
                dve.wait_ge(h_ready, i * NH + (n + 1) * DB)
                nc.vector.tensor_copy(carry[:, 1, n, :], h[:, n % 2, :, T - 1]).then_inc(carry_saved, 1)

            def sum_states(i, par, q):
                n, t = q // TT, q % TT
                if n == 0:
                    return
                dve.wait_ge(ht_ready, i * NHT + q + 1)
                if n == 1:
                    dve.wait_ge(acc_begun, i * TT + t + 1)
                else:
                    dve.wait_ge(acc_done, i * NSUM + q - 2 * TT + 1)
                nc.vector.scalar_tensor_tensor(out=acc[:, par, t, :], in0=ht[q % HT_BANKS][:, :],
                                               scalar=ct[:, par, t, n:n + 1], in1=acc[:, par, t, :],
                                               op0=ALU.mult, op1=ALU.add).then_inc(acc_done, 1)

            nc.vector.memset(carry[:, :, :, :], 0.0).then_inc(tiles_set, 1)
            nc.vector.memset(xin[:, :, T:T + 2 * HALO], 0.0).then_inc(tiles_set, 1)
            nc.vector.memset(wx_s[:, :, R:XB], 0.0).then_inc(tiles_set, 1)
            nc.vector.memset(wx_s[:, :, XB + NS:XC], 0.0).then_inc(tiles_set, 1)
            nc.vector.memset(ones_row[:, :], 0.0).then_inc(ones_set, 1)
            dve.wait_ge(ones_set, 1)
            nc.vector.memset(ones_row[0:XB, :], 1.0).then_inc(ones_set, 1)
            dve.wait_ge(ones_set, 2)
            nc.vector.memset(ones_row[0:R, :], 0.0).then_inc(ones_set, 1)
            dve.wait_ge(ones_set, 3)
            nc.vector.memset(eps_s[:, :], LN_EPS).then_inc(tiles_set, 1)
            nc.vector.memset(row_sum[:, :, :], 0.0).then_inc(res2_done, TT)
            dve.wait_ge(res2_done, TT)
            dve.wait_ge(tiles_set, 5)
            dve.wait_ge(ident_ready, 1)
            dve.wait_ge(conv_loaded, 32)
            for k in range(KCONV):
                rows = slice(k * GROUP, (k + 1) * GROUP)
                nc.vector.tensor_copy(eye[rows, :], ident[rows, rows]).then_inc(eye_ready, 1)
            dve.wait_ge(eye_ready, KCONV)
            for m in range(DB):
                for g in range(GROUPS):
                    nc.vector.tensor_scalar(taps[:, m, g, :], eye[:, :], convw_s[:, m, g:g + 1], None, ALU.mult)\
                        .then_inc(taps_ready, 1)
            dve.wait_ge(w_loaded, 16 * 4)
            for n, w in enumerate((wg_s, wu_s)):
                nc.vector.tensor_copy(w[:, :, :], integers(n).bitcast(I32)).then_inc(w_ready, 1)
            nc.vector.tensor_scalar(wd_s[:, :, :], wd_s[:, :, :].bitcast(I32), W_SCALE, None, ALU.mult)\
                .then_inc(w_ready, 1)
            dve.wait_ge(a_exp, 1)
            nc.vector.tensor_scalar(a_s[:, :, :], a_s[:, :, :], -1.0, None, ALU.mult).then_inc(a_ready, 1)
            for m in range(DB):
                times_u(dve, nc.vector, 0, 0, m)

            def step(i, par, j):
                first = isinstance(i, int) and i == 0
                if not first:
                    save_carry(i - 1, NS - 1)
                if j is not None and par == 0:
                    dve.wait_ge(carry_saved, i * NS)
                    nc.vector.tensor_copy(carry[:, 1, :, :], carry[:, bass.ds((j + 1) % 2, 1), :, :])\
                        .then_inc(carry_reset, 1)
                    dve.wait_ge(carry_reset, j + 1)
                for beat in range(NH):
                    scan(i, beat)
                    if beat >= DB and beat % DB == 1:
                        save_carry(i, beat // DB - 1)
                    if beat > DB:
                        sum_states(i, par, beat - DB - 1)
                    elif not first:
                        sum_states(i - 1, 1 - par, NHT - DB - 1 + beat)
                    if not (isinstance(i, int) and i < 2):
                        norms(i - 2, NH + beat)
                    if not first:
                        back(i - 1, 1 - par, beat)

            steps(dve, step)
            for q in range(NHT - DB - 1, NHT):
                sum_states(NCH - 1, (NCH - 1) % 2, q)
            for beat in range(NH):
                norms(NCH - 2, NH + beat)
                back(NCH - 1, (NCH - 1) % 2, beat)

def groups_apart(w):
    xin, res = w[:, :w.shape[1] // 2], w[:, w.shape[1] // 2:]
    xin = xin.reshape(w.shape[0], -1, KCONV, P // KCONV).swapaxes(2, 3).reshape(xin.shape)
    return np.concatenate([xin, res], axis=1)


def taps_first(w):
    group = P // KCONV
    return w.reshape(-1, group, KCONV).transpose(2, 1, 0).reshape(P, -1)


def kernel(L0_attn_x, L0_attn_W_in, L0_attn_conv_w, L0_attn_conv_b, L0_attn_W_x, L0_attn_W_dt, L0_attn_b_dt,
           L0_attn_A_log, L0_attn_D, L0_attn_W_out, L0_ffn_w_gate, L0_ffn_w_up, L0_ffn_w_down):
    import numpy as np
    import concourse.bacc as bacc
    from concourse import mybir as mb
    from concourse.bass_utils import run_bass_kernel_spmd

    x = np.ascontiguousarray(L0_attn_x)
    rows = x.reshape(-1, x.shape[-1])
    arrays = {
        "x": rows, "x_t": np.ascontiguousarray(rows.T),
        "w_in": groups_apart(np.asarray(L0_attn_W_in)), "conv_w": taps_first(np.asarray(L0_attn_conv_w)),
        "conv_b": np.asarray(L0_attn_conv_b).reshape(-1, P).T, "w_x": L0_attn_W_x,
        "w_dt": L0_attn_W_dt, "b_dt": L0_attn_b_dt, "a_log": L0_attn_A_log,
        "d_skip": np.asarray(L0_attn_D).reshape(-1, P).T, "w_out": L0_attn_W_out,
        "w_gate_t": np.asarray(L0_ffn_w_gate).T, "w_up_t": np.asarray(L0_ffn_w_up).T,
        "w_down_t": np.asarray(L0_ffn_w_down).T,
    }
    arrays = {name: np.ascontiguousarray(a) for name, a in arrays.items()}
    nc = bacc.Bacc("TRN2", target_bir_lowering=False, num_devices=1)
    args = [nc.dram_tensor(name, a.shape, mb.dt.from_np(a.dtype), kind="ExternalInput").ap()
            for name, a in arrays.items()]
    out = nc.dram_tensor("out", rows.shape, mb.dt.from_np(rows.dtype), kind="ExternalOutput").ap()
    mamba_swiglu(nc, *args, out)
    result = run_bass_kernel_spmd(nc, [arrays], core_ids=[0])
    return result.results[0]["out"].reshape(x.shape)
```
